# Optimizing a Trainium2 kernel written in Bass

```python
import numpy as np
import jax
import jax.numpy as jnp

def _softmax(x, axis=-1):
    return jax.nn.softmax(x, axis=axis)

def _gelu(x):
    return jax.nn.gelu(x, approximate=True)

def _silu(x):
    return jax.nn.silu(x)

def _sigmoid(x):
    return jax.nn.sigmoid(x)

def _layernorm(x, axis=-1, eps=1e-05):
    m = jnp.mean(x, axis=axis, keepdims=True)
    v = jnp.var(x, axis=axis, keepdims=True)
    return (x - m) / jnp.sqrt(v + eps)

def _scatter_add(tgt, idx, src, axis=0):
    return tgt.at[idx].add(src)

def _segment_sum(src, seg, n):
    return jax.ops.segment_sum(src, seg, n)
kernel_name = 'mk_decoder_postln_d1_seqx_r8_f3f241'

def setup_inputs(seed: int=0):
    np.random.seed(seed)
    _w = jnp.asarray

    def _rec_inputs():
        import jax
        import jax.numpy as jnp
        _rk = jax.random.key(seed)
        x = 0.0001212 + 1 * jax.random.normal(jax.random.fold_in(_rk, 1), (4, 256, 256), jnp.float32)
        _lenS = 256 - jax.random.randint(jax.random.fold_in(_rk, 7), (4,), 0, max(1, 256 // 4) + 1, jnp.int32)
        _lenS2 = 256 - jax.random.randint(jax.random.fold_in(_rk, 8), (4,), 0, max(1, 256 // 4) + 1, jnp.int32)
        _ctx_2048P = jax.random.normal(jax.random.fold_in(_rk, 11), (4, 16, 256), jnp.float32)
        _ctx_2048c = jax.random.dirichlet(jax.random.fold_in(_rk, 511), 0.3 * jnp.ones((16,), jnp.float32), (4, 256))
        _ctx_2048t = jnp.einsum('bsk,bkd->bsd', _ctx_2048c, _ctx_2048P)
        _ctx_2048t = _ctx_2048t * jax.lax.rsqrt(jnp.mean(jnp.square(_ctx_2048t)) + 1e-12) * 0.953939
        ctx_2048 = 0.000173663 + 1.0001 * (_ctx_2048t + 0.3 * jax.random.normal(jax.random.fold_in(_rk, 611), (4, 256, 256), jnp.float32))
        return (x, ctx_2048)
    x, ctx_2048 = _rec_inputs()

    def _L0_attn_setup():
        import jax, jax.numpy as jnp
        import numpy as np
        D_MODEL = 256
        N_HEADS = 32
        N_KV_HEADS = 8
        D_K = D_MODEL // N_HEADS
        REPS = N_HEADS // N_KV_HEADS
        B, S = (2, 256)
        key = jax.random.key(seed)
        ks = jax.random.split(key, 6)
        sd = 1.0 / np.sqrt(D_MODEL)
        return {'x': jax.random.normal(ks[0], (B, S, D_MODEL), jnp.float32), 'Wq': jax.random.normal(ks[1], (D_MODEL, N_HEADS * D_K), jnp.float32) * sd, 'bq': jnp.zeros((N_HEADS * D_K,), jnp.float32), 'Wk': jax.random.normal(ks[2], (D_MODEL, N_KV_HEADS * D_K), jnp.float32) * sd, 'bk': jnp.zeros((N_KV_HEADS * D_K,), jnp.float32), 'Wv': jax.random.normal(ks[3], (D_MODEL, N_KV_HEADS * D_K), jnp.float32) * sd, 'bv': jnp.zeros((N_KV_HEADS * D_K,), jnp.float32), 'Wo': jax.random.normal(ks[4], (N_HEADS * D_K, D_MODEL), jnp.float32) * sd, 'bo': jnp.zeros((D_MODEL,), jnp.float32)}
    _L0_attn_all = _L0_attn_setup()
    _L0_attn_in = {k: v for k, v in _L0_attn_all.items() if k in ('Wq', 'bq', 'Wk', 'bk', 'Wv', 'bv', 'Wo', 'bo')}
    del _L0_attn_all

    def _L0_xattn_setup():
        import jax, jax.numpy as jnp
        import numpy as np
        B_DIM, T_DIM, C_DIM = (16, 128, 256)

        def _wkv(w, u, k, v):
            Bn, Tn, Cn = k.shape
            NEG_INF = jnp.float32(-1e+38)

            def step(carry, kv_t):
                p, q, o = carry
                kt, vt = kv_t
                no = jnp.maximum(o, u + kt)
                A = jnp.exp(o - no)
                E = jnp.exp(u + kt - no)
                y = (A * p + E * vt) / (A * q + E)
                no2 = jnp.maximum(w + o, kt)
                A2 = jnp.exp(w + o - no2)
                E2 = jnp.exp(kt - no2)
                return ((A2 * p + E2 * vt, A2 * q + E2, no2), y)
            init = (jnp.zeros((Bn, Cn), k.dtype), jnp.zeros((Bn, Cn), k.dtype), jnp.full((Bn, Cn), NEG_INF, k.dtype))
            kT = jnp.moveaxis(k, 1, 0)
            vT = jnp.moveaxis(v, 1, 0)
            _, yT = jax.lax.scan(step, init, (kT, vT))
            return jnp.moveaxis(yT, 0, 1)
        key = jax.random.key(seed)
        k1, k2, k3, k4 = jax.random.split(key, 4)
        w = -jnp.exp(jax.random.normal(k1, (C_DIM,), jnp.float32))
        u = jax.random.normal(k2, (C_DIM,), jnp.float32)
        k = jax.random.normal(k3, (B_DIM, T_DIM, C_DIM), jnp.float32)
        v = jax.random.normal(k4, (B_DIM, T_DIM, C_DIM), jnp.float32)
        return {'B': B_DIM, 'T': T_DIM, 'C': C_DIM, 'w': w, 'u': u, 'k': k, 'v': v}
    _L0_xattn_all = _L0_xattn_setup()
    _L0_xattn_in = {k: v for k, v in _L0_xattn_all.items() if k in ('w', 'u')}
    del _L0_xattn_all

    def _L0_ffn_setup():
        import jax, jax.numpy as jnp
        import numpy as np
        HID = 256
        INTER = 1024
        NEXP = 8
        TOPK = 2
        EPS = 1e-05

        def _mock_fused_moe(x, selected_experts, routing_weights, expert_weight):
            y = jnp.einsum('bsh,hd->bsd', x, expert_weight)
            scale = routing_weights.sum(axis=-1, keepdims=True)
            return y * scale
        key = jax.random.key(seed)
        ks = jax.random.split(key, 6)
        s = lambda fan_in: 1.0 / np.sqrt(fan_in)
        return {'hidden_states': jax.random.normal(ks[0], (4, 512, HID), dtype=jnp.float32), 'gate_w': jax.random.uniform(ks[1], (HID, NEXP), jnp.float32, -s(HID), s(HID)), 'up_w': jax.random.uniform(ks[2], (HID, INTER), jnp.float32, -s(HID), s(HID)), 'down_w': jax.random.uniform(ks[3], (INTER, HID), jnp.float32, -s(INTER), s(INTER)), 'expert_weight': jax.random.normal(ks[4], (HID, HID), dtype=jnp.float32), 'ln_gamma': jnp.ones((HID,), jnp.float32), 'ln_beta': jnp.zeros((HID,), jnp.float32)}
    _L0_ffn_all = _L0_ffn_setup()
    _L0_ffn_in = {k: v for k, v in _L0_ffn_all.items() if k in ('gate_w', 'up_w', 'down_w', 'expert_weight', 'ln_gamma', 'ln_beta')}
    del _L0_ffn_all
    return {'x': x, 'ctx_2048': ctx_2048, 'L0_attn_Wq': _L0_attn_in['Wq'], 'L0_attn_bq': _L0_attn_in['bq'], 'L0_attn_Wk': _L0_attn_in['Wk'], 'L0_attn_bk': _L0_attn_in['bk'], 'L0_attn_Wv': _L0_attn_in['Wv'], 'L0_attn_bv': _L0_attn_in['bv'], 'L0_attn_Wo': _L0_attn_in['Wo'], 'L0_attn_bo': _L0_attn_in['bo'], 'L0_xattn_w': _L0_xattn_in['w'], 'L0_xattn_u': _L0_xattn_in['u'], 'L0_ffn_gate_w': _L0_ffn_in['gate_w'], 'L0_ffn_up_w': _L0_ffn_in['up_w'], 'L0_ffn_down_w': _L0_ffn_in['down_w'], 'L0_ffn_expert_weight': _L0_ffn_in['expert_weight'], 'L0_ffn_ln_gamma': _L0_ffn_in['ln_gamma'], 'L0_ffn_ln_beta': _L0_ffn_in['ln_beta']}

def reference(x, ctx_2048, L0_attn_Wq, L0_attn_bq, L0_attn_Wk, L0_attn_bk, L0_attn_Wv, L0_attn_bv, L0_attn_Wo, L0_attn_bo, L0_xattn_w, L0_xattn_u, L0_ffn_gate_w, L0_ffn_up_w, L0_ffn_down_w, L0_ffn_expert_weight, L0_ffn_ln_gamma, L0_ffn_ln_beta):
    import jax
    import jax.numpy as jnp

    def _L0_attn_ref(x, Wq, bq, Wk, bk, Wv, bv, Wo, bo):
        import jax, jax.numpy as jnp
        import numpy as np
        D_MODEL = 256
        N_HEADS = 32
        N_KV_HEADS = 8
        D_K = D_MODEL // N_HEADS
        REPS = N_HEADS // N_KV_HEADS
        B, S = (2, 256)
        b, s, _ = x.shape
        Q = (x @ Wq + bq).reshape(b, s, N_HEADS, D_K).transpose(0, 2, 1, 3)
        K = (x @ Wk + bk).reshape(b, s, N_KV_HEADS, D_K).transpose(0, 2, 1, 3)
        V = (x @ Wv + bv).reshape(b, s, N_KV_HEADS, D_K).transpose(0, 2, 1, 3)
        K = jnp.repeat(K, REPS, axis=1)
        V = jnp.repeat(V, REPS, axis=1)
        scores = jnp.einsum('bhqd,bhkd->bhqk', Q, K) / jnp.sqrt(jnp.float32(D_K))
        attn = jax.nn.softmax(scores, axis=-1)
        out = jnp.einsum('bhqk,bhkd->bhqd', attn, V)
        out = out.transpose(0, 2, 1, 3).reshape(b, s, N_HEADS * D_K)
        return out @ Wo + bo

    def _L0_xattn_ref(B, T, C, w, u, k, v):
        import jax, jax.numpy as jnp
        import numpy as np
        B_DIM, T_DIM, C_DIM = (16, 128, 256)

        def _wkv(w, u, k, v):
            Bn, Tn, Cn = k.shape
            NEG_INF = jnp.float32(-1e+38)

            def step(carry, kv_t):
                p, q, o = carry
                kt, vt = kv_t
                no = jnp.maximum(o, u + kt)
                A = jnp.exp(o - no)
                E = jnp.exp(u + kt - no)
                y = (A * p + E * vt) / (A * q + E)
                no2 = jnp.maximum(w + o, kt)
                A2 = jnp.exp(w + o - no2)
                E2 = jnp.exp(kt - no2)
                return ((A2 * p + E2 * vt, A2 * q + E2, no2), y)
            init = (jnp.zeros((Bn, Cn), k.dtype), jnp.zeros((Bn, Cn), k.dtype), jnp.full((Bn, Cn), NEG_INF, k.dtype))
            kT = jnp.moveaxis(k, 1, 0)
            vT = jnp.moveaxis(v, 1, 0)
            _, yT = jax.lax.scan(step, init, (kT, vT))
            return jnp.moveaxis(yT, 0, 1)
        return _wkv(w, u, k, v)

    def _L0_ffn_ref(hidden_states, gate_w, up_w, down_w, expert_weight, ln_gamma, ln_beta):
        import jax, jax.numpy as jnp
        import numpy as np
        HID = 256
        INTER = 1024
        NEXP = 8
        TOPK = 2
        EPS = 1e-05

        def _mock_fused_moe(x, selected_experts, routing_weights, expert_weight):
            y = jnp.einsum('bsh,hd->bsd', x, expert_weight)
            scale = routing_weights.sum(axis=-1, keepdims=True)
            return y * scale
        residuals = hidden_states
        logits = jnp.einsum('bsh,he->bse', hidden_states, gate_w)
        routing_weights, selected_experts = jax.lax.top_k(logits, TOPK)
        h = jnp.einsum('bsh,hi->bsi', residuals, up_w)
        h = jnp.square(jax.nn.relu(h))
        shared_out = jnp.einsum('bsi,ih->bsh', h, down_w)
        moe_out = _mock_fused_moe(hidden_states, selected_experts, routing_weights, expert_weight)
        y = shared_out + moe_out
        mu = y.mean(axis=-1, keepdims=True)
        var = jnp.mean(jnp.square(y - mu), axis=-1, keepdims=True)
        return (y - mu) * jax.lax.rsqrt(var + EPS) * ln_gamma + ln_beta
    x = _layernorm(x + _L0_attn_ref(x, L0_attn_Wq, L0_attn_bq, L0_attn_Wk, L0_attn_bk, L0_attn_Wv, L0_attn_bv, L0_attn_Wo, L0_attn_bo), axis=-1)
    x = _layernorm(x + _L0_xattn_ref(4, 256, 256, L0_xattn_w, L0_xattn_u, x, ctx_2048), axis=-1)
    x = _layernorm(x + _L0_ffn_ref(x, L0_ffn_gate_w, L0_ffn_up_w, L0_ffn_down_w, L0_ffn_expert_weight, L0_ffn_ln_gamma, L0_ffn_ln_beta), axis=-1)
    return x

_drawn_inputs = setup_inputs


def setup_inputs(seed=0):
    import zlib

    import numpy as np

    out = dict(_drawn_inputs(seed))
    spreads = {'L0_attn_bq': (0.0, 0.679),
     'L0_attn_bk': (0.0, 0.8),
     'L0_attn_bv': (0.0, 0.1),
     'L0_attn_bo': (0.0, 0.1),
     'L0_ffn_ln_gamma': (1.0, 0.2),
     'L0_ffn_ln_beta': (0.0, 0.1)}
    factors = {}
    for name, (base, spread) in spreads.items():
        noise = np.random.default_rng([zlib.crc32(name.encode()), seed]).standard_normal(out[name].shape)
        drawn = base * np.exp(spread * noise) if base else spread * noise
        out[name] = jnp.asarray(drawn.astype(out[name].dtype))
    for name, factor in factors.items():
        out[name] = (out[name] * factor).astype(out[name].dtype)
    return out
```

```python
import concourse.bass as bass
from concourse import mybir
from contextlib import ExitStack
import numpy as np


def decoder_layer(nc, x, ctx, wq, bq, wk, bk, wv, bv, wo, bo, w_decay, u_bonus,
                  gate_w, up_w, down_w, expert_w, ln_gamma, ln_beta, out):
    fp32, bf16 = mybir.dt.float32, mybir.dt.bfloat16
    ALU = mybir.AluOpType
    ACT = mybir.ActivationFunctionType
    AX = mybir.AxisListType.X

    B, T, D = x.shape
    P = 128
    TT = T // P
    CT = D // P
    KVD = wk.shape[1]
    HD = 8
    NG = KVD // HD
    REP = D // KVD
    GS = 4
    NSET = NG // GS
    HS = GS * REP
    PARTS = 3
    BLOCKS = [(0, 0), (1, 0), (0, 1), (1, 1), (2, 0), (0, 2)]
    QK = len(BLOCKS) * HD
    QKM = QK + PARTS
    SCALE = float(np.float32(1.0) / np.sqrt(np.float32(HD)))
    NI = up_w.shape[1] // P
    NE = gate_w.shape[1]
    EPS = 1e-5
    NEG = -1e38
    UNITS = 16
    W2 = TT * D

    PERIOD = NSET * UNITS
    XT, QP, KV = -30, -29, -28
    SPLIT = -27
    ROWS = (-24, -11)
    CTXT = -18
    MAXIMA = -UNITS
    MROWS = 0
    EXP = 5
    PV_LAG, OT_LAG = 2, 2
    AOT, OP, LN1 = 45, 47, 48
    X1T = 51
    WKV = 52
    YT = 66
    LN2 = 67
    X2T, GATE, EXPERT, UP = 70, 71, 72, 74
    DOWN = 82
    LN3, LN4 = 84, 87
    STORE = 90
    TICKS = range(XT, (B - 1) * PERIOD + STORE + 1)

    ectx = ExitStack()
    with ectx:
        def sb(name, shape, dt=fp32):
            return ectx.enter_context(nc.sbuf_tensor(name, shape, dt))

        def ps(name, shape, dt=fp32):
            return ectx.enter_context(nc.psum_tensor(name, shape, dt))

        def sem(name):
            return ectx.enter_context(nc.semaphore(name))

        wq_sb = sb("wq_sb", [P, CT, D])
        wk_sb = sb("wk_sb", [P, CT, KVD])
        wq_cols = sb("wq_cols", [P, CT, D])
        wk_cols = sb("wk_cols", [P, CT, KVD])
        wv_sb = sb("wv_sb", [P, CT, KVD])
        wo_sb = sb("wo_sb", [P, CT, D])
        up_sb = sb("up_sb", [P, CT, NI * P])
        down_sb = sb("down_sb", [P, NI, D])
        expert_sb = sb("expert_sb", [P, CT, D])
        gate_sb = sb("gate_sb", [P, CT, NE])
        bq_sb = sb("bq_sb", [P, NSET])
        bk_sb = sb("bk_sb", [KVD, 1])
        bv_sb = sb("bv_sb", [P, KVD])
        bo_sb = sb("bo_sb", [P, D])
        decay_sb = sb("decay_sb", [P, CT])
        bonus_sb = sb("bonus_sb", [P, CT])
        gamma_sb = sb("gamma_sb", [P, D])
        beta_sb = sb("beta_sb", [P, D])
        ident = sb("ident", [P, P])
        ident_bf = sb("ident_bf", [P, P], bf16)
        minus_half = sb("minus_half", [P, TT])

        x_in = [sb(f"x_in{b}", [P, TT, D]) for b in range(B)]
        ctx_in = [sb(f"ctx_in{b}", [P, TT, D]) for b in range(B)]
        x_t = sb("x_t", [P, CT, T])
        ctx_t = [sb(f"ctx_t{i}", [P, CT, T]) for i in range(3)]
        q_parts = sb("q_parts", [P, NSET, PARTS, T], bf16)
        q_rest = sb("q_rest", [P, NSET, T])
        k_parts = sb("k_parts", [KVD, PARTS, T], bf16)
        k_rest = sb("k_rest", [KVD, T])
        q_rows = [sb(f"q_rows{i}", [64, HS, T], bf16) for i in range(3)]
        k_rows = [sb(f"k_rows{i}", [64, NG, T], bf16) for i in range(2)]
        v_cols = [sb(f"v_cols{i}", [P, TT, NG, 32]) for i in range(3)]
        neg_max = [sb(f"neg_max{i}", [P, TT, HS]) for i in range(2)]
        max_rest = sb("max_rest", [P, TT, HS])
        max_parts = sb("max_parts", [P, TT, PARTS, HS], bf16)
        max_t = sb("max_t", [PARTS * HS, T], bf16)
        probs = [sb(f"probs{i}", [P, 2 * T]) for i in range(8)]
        heads_t = [sb(f"heads_t{i}", [P, 2 * T]) for i in range(2)]
        inv_sum = [sb(f"inv_sum{i}", [P, 2, TT, GS]) for i in range(2)]
        att = sb("att", [P, TT, D])
        att_t = sb("att_t", [P, CT, T])
        x_bo = sb("x_bo", [P, TT, D])
        h1 = sb("h1", [P, TT, D])
        x1 = sb("x1", [P, TT, D])
        x1_t = sb("x1_t", [P, CT, T])
        top = sb("top", [P, CT, T + 1])
        num = sb("num", [P, CT, T + 1])
        den = sb("den", [P, CT, T + 1])
        arg = sb("arg", [P, 4, CT, T])
        wgt = sb("wgt", [P, 4, CT, T])
        gap = sb("gap", [P, CT, T])
        new_v = sb("new_v", [P, 2, CT, T])
        y_num = sb("y_num", [P, CT, T])
        y_old = sb("y_old", [P, CT, T])
        y_den = sb("y_den", [P, CT, T])
        y_inv = sb("y_inv", [P, CT, T])
        y_t = sb("y_t", [P, CT, T])
        h2 = sb("h2", [P, TT, D])
        x2 = [sb(f"x2_{i}", [P, TT, D]) for i in range(2)]
        x2_beta = sb("x2_beta", [P, TT, D])
        x2_t = sb("x2_t", [P, CT, T])
        top8 = sb("top8", [P, TT, 8])
        route = sb("route", [P, TT])
        expert_out = sb("expert_out", [P, TT, D])
        relu_t = [sb(f"relu_t{i}", [P, 2, T]) for i in range(2)]
        inner_t = sb("inner_t", [P, NI, T])
        h3 = sb("h3", [P, TT, D])
        h3g = sb("h3g", [P, TT, D])
        h4 = sb("h4", [P, TT, D])
        y_out = sb("y_out", [P, TT, D])
        stats = [sb(f"stats{i}", [P, TT, 6]) for i in range(4)]
        mean_var = [sb(f"mean_var{i}", [P, TT, 2]) for i in range(4)]
        var_eps = [sb(f"var_eps{i}", [P, TT]) for i in range(4)]
        rstd = [sb(f"rstd{i}", [P, TT]) for i in range(4)]

        ps_max = [ps(f"ps_max{i}", [P, 2, T]) for i in range(2)]
        ps_exp = [ps(f"ps_exp{i}", [P, 2 * T]) for i in range(2)]
        ps_heads = [ps(f"ps_heads{i}", [P, 2 * T]) for i in range(2)]
        ps_a = ps("ps_a", [P, 2 * T])
        ps_b = ps("ps_b", [P, 2 * T])
        ps_a_bf = ps_a[:, 0:T].bitcast(bf16)

        s_w_att = sem("s_w_att")
        s_wcols = sem("s_wcols")
        s_w_post = sem("s_w_post")
        s_x = [sem(f"s_x_in{b}") for b in range(B)]
        s_ctx = [sem(f"s_ctx_in{b}") for b in range(B)]
        s_ident = sem("s_ident")
        s_const = sem("s_const")
        s_a = sem("s_a")
        s_a_free = sem("s_a_free")
        s_b = sem("s_b")
        s_b_free = sem("s_b_free")
        s_qk1 = sem("s_qk1")
        s_rest = sem("s_rest")
        s_qk = sem("s_qk")
        s_v = sem("s_v")
        s_rows = [sem(f"s_rows{i}") for i in range(3)]
        s_krows = [sem(f"s_krows{i}") for i in range(2)]
        s_max_mm = sem("s_max_mm")
        s_max = sem("s_max")
        s_mparts = sem("s_mparts")
        s_maxt = sem("s_maxt")
        s_mrows = [sem(f"s_mrows{i}") for i in range(3)]
        s_exp_mm = sem("s_exp_mm")
        s_exp = sem("s_exp")
        s_pv = sem("s_pv")
        s_heads = sem("s_heads")
        s_att = sem("s_att")
        s_xbo = sem("s_xbo")
        s_var = sem("s_var")
        s_rstd = sem("s_rstd")
        s_x1 = sem("s_x1")
        s_arg = sem("s_arg")
        s_wgt = sem("s_wgt")
        s_newv = sem("s_newv")
        s_state = sem("s_state")
        s_ynum = sem("s_ynum")
        s_y = sem("s_y")
        s_x2 = sem("s_x2")
        s_x2b = sem("s_x2b")
        s_route = sem("s_route")
        s_eout = sem("s_eout")
        s_relu = sem("s_relu")
        s_inner = sem("s_inner")
        s_out = sem("s_out")
        s_store = sem("s_store")
        s_vec = sem("s_vec")
        s_pool = sem("s_pool")
        s_act = sem("s_act")

        def flat(ap):
            return ap.rearrange("p a b -> p (a b)")

        def row(ap):
            return ap.rearrange("(a n) -> a n", a=1)

        def uses_of_a():
            order = []
            for tick in TICKS:
                for b in range(B):
                    t = tick - b * PERIOD
                    for name, at in (("x", XT), ("q", QP), ("kv", KV), ("ctx", CTXT), ("att", AOT), ("op", OP),
                                     ("x1", X1T), ("y", YT), ("x2", X2T), ("gate", GATE)):
                        if t == at:
                            order.append((name, b, 0))
                    for g in range(NSET):
                        if t == MROWS + g * UNITS:
                            order.append(("m", b, g))
                        for n in range(2):
                            if t == EXP + g * UNITS + 8 * n + 8 + PV_LAG + OT_LAG:
                                order.append(("heads", b, 2 * g + n))
            return {use: i for i, use in enumerate(order)}

        A_USE = uses_of_a()

        def in_order(steps):
            order = [(name, b) for tick in TICKS for b in range(B) for name, at in steps if tick - b * PERIOD == at]
            return {step: i for i, step in enumerate(order)}

        A_COPIES = in_order((("x", XT), ("ctx", CTXT), ("att", AOT), ("x1", X1T), ("x2", X2T)))
        VAR_AT = in_order(((0, LN1), (1, LN2), (2, LN3), (3, LN4)))
        B_USE = in_order((("expert", EXPERT), *((f"up{i}", UP + i) for i in range(0, NI, 2)), ("down", DOWN)))
        B_DOWN = [B_USE["down", b] for b in range(B)]

        def heads_tick(g, n):
            return EXP + g * UNITS + 8 * n + 8 + PV_LAG + OT_LAG

        block = ectx.enter_context(nc.Block())

        @block.sync
        def _(sp):
            def token_tiles(a):
                return a.rearrange("(t p) c -> p t c", p=P)

            sp.dma_start(x_in[0][:], token_tiles(x[0])).then_inc(s_x[0], 16)
            sp.dma_start(wq_sb[:], token_tiles(wq)).then_inc(s_w_att, 16)
            sp.dma_start(wk_sb[:], token_tiles(wk)).then_inc(s_w_att, 16)
            sp.dma_start(wv_sb[:], token_tiles(wv)).then_inc(s_w_att, 16)
            for g in range(NSET):
                sp.dma_start(bq_sb[:, g:g + 1], bq[g * P:g * P + P].rearrange("(h d) -> d h", d=HD),
                             allow_slow_non_contiguous=True).then_inc(s_w_att, 16)
            sp.dma_start(bk_sb[:], bk.rearrange("(h d) -> d h", d=HD),
                         allow_slow_non_contiguous=True).then_inc(s_w_att, 16)
            sp.dma_start(bv_sb[:], row(bv).broadcast_to([P, KVD])).then_inc(s_w_att, 16)

            def rows_of_set(b, g):
                s = NSET * b + g
                sp.wait_ge(s_qk, b + 1)
                if s >= 3:
                    sp.wait_ge(s_exp_mm, UNITS * (s - 2))
                for r, (qp, kp) in enumerate(BLOCKS):
                    sp.dma_start(q_rows[s % 3][HD * r:HD * r + HD, :, :],
                                 q_parts[:, g, qp, :]).then_inc(s_rows[s % 3], 16)
                    if g == 0:
                        if r == 0 and b >= 2:
                            sp.wait_ge(s_exp_mm, UNITS * NSET * (b - 1))
                        if r == 0:
                            sp.wait_ge(s_const, 2)
                        sp.dma_start(k_rows[b % 2][HD * r:HD * r + HD, :, :],
                                     k_parts[:, kp, :]).then_inc(s_krows[b % 2], 16)

            for tick in TICKS:
                for b in range(B):
                    t = tick - b * PERIOD
                    for g in range(NSET):
                        if t == ROWS[g]:
                            rows_of_set(b, g)
                        if t == MROWS + g * UNITS + 1:
                            s = NSET * b + g
                            sp.wait_ge(s_maxt, s + 1)
                            sp.dma_start(q_rows[s % 3][QK:QKM, :, :],
                                         max_t[:, :]).then_inc(s_mrows[s % 3], 16)
                    if t == STORE:
                        sp.wait_ge(s_out, b + 1)
                        sp.dma_start(token_tiles(out[b]), y_out[:]).then_inc(s_store, 16)
                if tick == ROWS[0]:
                    for b in range(1, B):
                        sp.dma_start(x_in[b][:], token_tiles(x[b])).then_inc(s_x[b], 16)
                    for b in range(B):
                        sp.dma_start(ctx_in[b][:], token_tiles(ctx[b])).then_inc(s_ctx[b], 16)
                    for dst, src in ((wo_sb, wo), (up_sb, up_w), (down_sb, down_w), (expert_sb, expert_w),
                                     (gate_sb, gate_w)):
                        sp.dma_start(dst[:], token_tiles(src)).then_inc(s_w_post, 16)
                    for dst, src in ((bo_sb, bo), (gamma_sb, ln_gamma), (beta_sb, ln_beta)):
                        sp.dma_start(dst[:], row(src).broadcast_to([P, D])).then_inc(s_w_post, 16)
                    for dst, src in ((decay_sb, w_decay), (bonus_sb, u_bonus)):
                        sp.dma_start(dst[:], src.rearrange("(c p) -> p c", p=P),
                                     allow_slow_non_contiguous=True).then_inc(s_w_post, 16)
            sp.wait_ge(s_store, 16 * B)

        @block.tensor
        def _(pe):
            use_b = [0]
            ps_a_tiles = ps_a[:, :].rearrange("p (c t) -> p c t", c=CT)

            def open_a(use):
                if A_USE[use] >= 1:
                    pe.wait_ge(s_a_free, A_USE[use])

            def open_b():
                if use_b[0] >= 1:
                    pe.wait_ge(s_b_free, use_b[0])
                use_b[0] += 1

            def transposes(src, cast_in=None):
                for c in range(CT):
                    for i in range(TT):
                        last = nc.tensor.transpose(ps_a[:, c * T + i * P:c * T + i * P + P],
                                                   src[:, i, c * P:c * P + P], ident[:, :])
                last.then_inc(s_a, 1)

            def maxima_unit(b, g, i):
                s, n = NSET * b + g, UNITS * (NSET * b + g) + i
                j, qt, half = i // 4, (i // 2) % 2, i % 2
                if i == 0:
                    pe.wait_ge(s_rows[s % 3], 16 * len(BLOCKS) * (s // 3 + 1))
                    if g == 0:
                        pe.wait_ge(s_krows[b % 2], 16 * len(BLOCKS) * (b // 2 + 1))
                if n >= 2:
                    pe.wait_ge(s_max, n - 1)
                for r in range(2):
                    last = nc.tensor.matmul(ps_max[n % 2][:, r, :],
                                            q_rows[s % 3][0:QK, REP * j + 2 * half + r, qt * P:qt * P + P],
                                            k_rows[b % 2][0:QK, GS * g + j, :], start=True, stop=True)
                last.then_inc(s_max_mm, 1)

            def exp_unit(b, g, i):
                s, n = NSET * b + g, UNITS * (NSET * b + g) + i
                pair, kt, j = i // 8, (i // 4) % 2, i % 4
                if i == 0:
                    pe.wait_ge(s_mrows[s % 3], 16 * (s // 3 + 1))
                if n >= 2:
                    pe.wait_ge(s_exp, n - 1)
                nc.tensor.matmul(ps_exp[n % 2][:, :], k_rows[b % 2][0:QKM, GS * g + j, kt * P:kt * P + P],
                                 q_rows[s % 3][0:QKM, REP * j + 2 * pair:REP * j + 2 * pair + 2, :]
                                 .rearrange("p h t -> p (h t)"), start=True, stop=True).then_inc(s_exp_mm, 1)

            def pv_group(b, g, i):
                s, n = NSET * b + g, 4 * (NSET * b + g) + i
                pair, kt = i // 2, i % 2
                if i == 0 and g == 0:
                    pe.wait_ge(s_v, b + 1)
                pe.wait_ge(s_exp, 4 * n + 4)
                if kt == 0 and s >= 1:
                    pe.wait_ge(s_heads, 2 * (s - 1) + pair + 1)
                for j in range(GS):
                    last = nc.tensor.matmul(ps_heads[pair][32 * j:32 * j + 32, :],
                                            v_cols[b % 3][:, kt, GS * g + j, :], probs[(4 * n + j) % 8][:, :],
                                            start=(kt == 0), stop=(kt == 1))
                last.then_inc(s_pv, 1)

            pe.wait_ge(s_ident, 2)
            for tick in TICKS:
                for b in range(B):
                    t = tick - b * PERIOD
                    if t == XT:
                        pe.wait_ge(s_x[b], 16)
                        open_a(("x", b, 0))
                        transposes(x_in[b])
                    if t == QP:
                        if b == 0:
                            pe.wait_ge(s_w_att, 16 * 7)
                        if b == 0:
                            pe.wait_ge(s_wcols, 2 * CT)
                        open_a(("q", b, 0))
                        pe.wait_ge(s_act, A_COPIES["x", b] + 1)
                        for g in range(NSET):
                            for c in range(CT):
                                last = nc.tensor.matmul(ps_a_tiles[:, g, :], wq_cols[:, c, g * P:g * P + P],
                                                        x_t[:, c, :], start=(c == 0), stop=(c == CT - 1))
                        last.then_inc(s_a, 1)
                    if t == KV:
                        open_a(("kv", b, 0))
                        for c in range(CT):
                            nc.tensor.matmul(ps_a[0:KVD, 0:T], wk_cols[:, c, :], x_t[:, c, :],
                                             start=(c == 0), stop=(c == CT - 1))
                        for i in range(TT):
                            for c in range(CT):
                                last = nc.tensor.matmul(ps_a[:, T + i * KVD:T + i * KVD + KVD],
                                                        x_t[:, c, i * P:i * P + P], wv_sb[:, c, :],
                                                        start=(c == 0), stop=(c == CT - 1))
                        last.then_inc(s_a, 1)
                    if t == CTXT:
                        pe.wait_ge(s_ctx[b], 16)
                        open_a(("ctx", b, 0))
                        transposes(ctx_in[b])
                    for g in range(NSET):
                        if t == MROWS + g * UNITS:
                            s = NSET * b + g
                            open_a(("m", b, g))
                            pe.wait_ge(s_mparts, s + 1)
                            for i in range(TT):
                                last = nc.tensor.transpose(ps_a_bf[0:PARTS * HS, i * P:i * P + P],
                                                           max_parts[:, i, :, :].rearrange("p a b -> p (a b)"),
                                                           ident_bf[:, :])
                            last.then_inc(s_a, 1)
                        i = t - EXP - g * UNITS
                        if 0 <= i < UNITS:
                            exp_unit(b, g, i)
                    for g in range(NSET):
                        i = t - MAXIMA - g * UNITS
                        if 0 <= i < UNITS:
                            maxima_unit(b, g, i)
                        i = t - EXP - g * UNITS - 3 - PV_LAG
                        if i in (0, 4, 8, 12):
                            pv_group(b, g, i // 4)
                        for pair in range(2):
                            if t == heads_tick(g, pair):
                                open_a(("heads", b, 2 * g + pair))
                                pe.wait_ge(s_heads, 2 * (NSET * b + g) + pair + 1)
                                for i in range(4):
                                    last = nc.tensor.transpose(ps_a[:, i * P:i * P + P],
                                                               heads_t[pair][:, i * P:i * P + P], ident[:, :])
                                last.then_inc(s_a, 1)
                    if t == AOT:
                        open_a(("att", b, 0))
                        pe.wait_ge(s_att, 2 * NSET * (b + 1))
                        transposes(att)
                    if t == OP:
                        if b == 0:
                            pe.wait_ge(s_w_post, 16 * 10)
                        open_a(("op", b, 0))
                        pe.wait_ge(s_act, A_COPIES["att", b] + 1)
                        for i in range(TT):
                            for c in range(CT):
                                last = nc.tensor.matmul(ps_a[:, i * D:i * D + D], att_t[:, c, i * P:i * P + P],
                                                        wo_sb[:, c, :], start=(c == 0), stop=(c == CT - 1))
                        last.then_inc(s_a, 1)
                    if t == X1T:
                        open_a(("x1", b, 0))
                        pe.wait_ge(s_x1, b + 1)
                        transposes(x1)
                    if t == YT:
                        open_a(("y", b, 0))
                        pe.wait_ge(s_y, b + 1)
                        transposes(y_t)
                    if t == X2T:
                        open_a(("x2", b, 0))
                        pe.wait_ge(s_x2, b + 1)
                        transposes(x2[b % 2])
                    if t == GATE:
                        open_a(("gate", b, 0))
                        pe.wait_ge(s_act, A_COPIES["x2", b] + 1)
                        for i in range(TT):
                            for c in range(CT):
                                last = nc.tensor.matmul(ps_a[:, i * NE:i * NE + NE], x2_t[:, c, i * P:i * P + P],
                                                        gate_sb[:, c, :], start=(c == 0), stop=(c == CT - 1))
                        last.then_inc(s_a, 1)
                    if t == EXPERT:
                        open_b()
                        for i in range(TT):
                            for c in range(CT):
                                last = nc.tensor.matmul(ps_b[:, i * D:i * D + D], x2_t[:, c, i * P:i * P + P],
                                                        expert_sb[:, c, :], start=(c == 0), stop=(c == CT - 1))
                        last.then_inc(s_b, 1)
                    if UP <= t < UP + NI and (t - UP) % 2 == 0:
                        open_b()
                        for i in range(2):
                            for c in range(CT):
                                m = t - UP + i
                                last = nc.tensor.matmul(ps_b[:, i * T:i * T + T], up_sb[:, c, m * P:m * P + P],
                                                        x2_t[:, c, :], start=(c == 0), stop=(c == CT - 1))
                        last.then_inc(s_b, 1)
                    if t == DOWN:
                        open_b()
                        for i in range(TT):
                            for m in range(NI):
                                if i == 0 and m % 2 == 0:
                                    pe.wait_ge(s_inner, NI // 2 * b + m // 2 + 1)
                                last = nc.tensor.matmul(ps_b[:, i * D:i * D + D], inner_t[:, m, i * P:i * P + P],
                                                        down_sb[:, m, :], start=(m == 0), stop=(m == NI - 1))
                        last.then_inc(s_b, 1)

        @block.scalar
        def _(act):
            use_b = [0]

            def copy_a(use, dst):
                act.wait_ge(s_a, A_USE[use] + 1)
                nc.scalar.activation(dst, ps_a[:, :], ACT.Copy).then_inc(s_a_free, 1)

            nact = [0]

            def evacuate(name, b, dst):
                act.wait_ge(s_a, A_USE[name, b, 0] + 1)
                assert A_COPIES[name, b] == nact[0]
                nc.scalar.activation(dst, ps_a[:, :], ACT.Copy).then_inc(s_act, 1)
                nact[0] += 1
                act.wait_ge(s_act, nact[0])
                act.sem_inc(s_a_free, 1)

            for tick in TICKS:
                for b in range(B):
                    t = tick - b * PERIOD
                    if t == XT:
                        evacuate("x", b, flat(x_t[:, :, :]))
                    if t == QP:
                        act.wait_ge(s_a, A_USE["q", b, 0] + 1)
                        if b == 0:
                            act.wait_ge(s_w_att, 16 * 7)
                        if b >= 1:
                            act.wait_ge(s_rows[(NSET * b - 1) % 3], 16 * len(BLOCKS) * ((NSET * b - 1) // 3 + 1))
                            act.wait_ge(s_rows[(NSET * b - 2) % 3], 16 * len(BLOCKS) * ((NSET * b - 2) // 3 + 1))
                            act.wait_ge(s_krows[(b - 1) % 2], 16 * len(BLOCKS) * ((b - 1) // 2 + 1))
                        for g in range(NSET):
                            nc.scalar.activation(q_parts[:, g, 0, :], ps_a[:, g * T:g * T + T], ACT.Identity,
                                                 bias=bq_sb[:, g:g + 1]).then_inc(s_qk1, 1)
                    if t == KV:
                        act.wait_ge(s_a, A_USE["kv", b, 0] + 1)
                        nc.scalar.activation(k_parts[:, 0, :], ps_a[0:KVD, 0:T], ACT.Identity,
                                             bias=bk_sb[:, 0:1]).then_inc(s_qk1, 1)
                    if t == CTXT:
                        if b >= 3:
                            act.wait_ge(s_newv, b - 2)
                        evacuate("ctx", b, flat(ctx_t[b % 3][:, :, :]))
                    for g in range(NSET):
                        i = t - EXP - g * UNITS
                        if 0 <= i < UNITS:
                            n = UNITS * (NSET * b + g) + i
                            act.wait_ge(s_exp_mm, n + 1)
                            if n >= 8:
                                act.wait_ge(s_pv, (n - 8) // 4 + 1)
                            nc.scalar.activation(probs[n % 8][:, :], ps_exp[n % 2][:, :], ACT.Exp,
                                                 scale=SCALE).then_inc(s_exp, 1)
                    for g in range(NSET):
                        for pair in range(2):
                            if t == heads_tick(g, pair):
                                n = 2 * (NSET * b + g) + pair
                                act.wait_ge(s_pv, 2 * n + 2)
                                if n >= 2:
                                    act.wait_ge(s_att, n - 1)
                                nc.scalar.activation(heads_t[pair][:, :], ps_heads[pair][:, :],
                                                     ACT.Copy).then_inc(s_heads, 1)
                    if t == AOT:
                        evacuate("att", b, flat(att_t[:, :, :]))
                    if t == X1T:
                        if b >= 1:
                            act.wait_ge(s_arg, 2 * b)
                        evacuate("x1", b, flat(x1_t[:, :, :]))
                    if t in (WKV + 3, WKV + 4):
                        half = t - WKV - 3
                        act.wait_ge(s_arg, 2 * b + half + 1)
                        if b >= 1:
                            act.wait_ge(s_y, b)
                        nc.scalar.activation(wgt[:, 2 * half:2 * half + 2].rearrange("p a c t -> p (a c t)"),
                                             arg[:, 2 * half:2 * half + 2].rearrange("p a c t -> p (a c t)"),
                                             ACT.Exp).then_inc(s_wgt, 1)
                    if t == X2T:
                        evacuate("x2", b, flat(x2_t[:, :, :]))
                    if t == EXPERT + 1:
                        act.wait_ge(s_b, use_b[0] + 1)
                        use_b[0] += 1
                        act.wait_ge(s_route, b + 1)
                        for i in range(TT):
                            ins = nc.scalar.activation(expert_out[:, i, :], ps_b[:, i * D:i * D + D], ACT.Copy,
                                                       scale=route[:, i:i + 1])
                            ins.then_inc(s_eout, 1)
                        act.wait_ge(s_eout, TT * (b + 1))
                        act.sem_inc(s_b_free, 1)
                    if UP < t <= UP + NI and (t - UP) % 2 == 1:
                        n = NI // 2 * b + (t - UP) // 2
                        act.wait_ge(s_b, use_b[0] + 1)
                        use_b[0] += 1
                        if n >= 2:
                            act.wait_ge(s_inner, n - 1)
                        nc.scalar.activation(flat(relu_t[n % 2][:, :, :]), ps_b[:, :], ACT.Relu).then_inc(s_relu, 1)
                        act.wait_ge(s_relu, n + 1)
                        act.sem_inc(s_b_free, 1)
                    if t == DOWN + 1:
                        use_b[0] += 1

        @block.gpsimd
        def _(gp):
            npool = [0]

            def own(ins):
                ins.then_inc(s_pool, 1)
                npool[0] += 1
                gp.wait_ge(s_pool, npool[0])

            own(gp.memset(ident[:], 0.0))
            gp.affine_select(out=ident[:], in_=ident[:], compare_op=ALU.not_equal, fill=1.0, base=0,
                             pattern=[[-1, P]], channel_multiplier=1).then_inc(s_ident, 1)
            gp.wait_ge(s_ident, 1)
            gp.tensor_copy(ident_bf[:], ident[:]).then_inc(s_ident, 1)
            for i in range(2):
                gp.memset(k_rows[i][:], 1.0).then_inc(s_const, 1)
            for i in range(3):
                own(gp.memset(v_cols[i][:], 0.0))
                gp.memset(v_cols[i][:, :, :, HD:HD + 1], 1.0).then_inc(s_const, 1)
            gp.memset(minus_half[:], -0.5).then_inc(s_const, 1)
            gp.memset(top[:, :, 0:1], NEG).then_inc(s_const, 1)
            gp.memset(num[:, :, 0:1], 0.0).then_inc(s_const, 1)
            gp.memset(den[:, :, 0:1], 0.0).then_inc(s_const, 1)
            gp.wait_ge(s_const, 9)

            def power(k, n):
                gp.wait_ge(s_var, n)
                gp.tensor_tensor(rstd[k][:], var_eps[k][:], minus_half[:], ALU.pow).then_inc(s_rstd, 1)

            nln = [0]
            for tick in TICKS:
                for b in range(B):
                    t = tick - b * PERIOD
                    if t == SPLIT:
                        gp.wait_ge(s_rest, 3 * (b + 1))
                        own(gp.tensor_copy(q_parts[:, :, 1, :], q_rest[:, :, :]))
                        gp.tensor_copy(k_parts[:, 1, :], k_rest[:, :]).then_inc(s_pool, 1)
                        npool[0] += 1
                        gp.tensor_tensor(q_parts[:, :, 2, :], q_rest[:, :, :], q_parts[:, :, 1, :],
                                         ALU.subtract).then_inc(s_pool, 1)
                        npool[0] += 1
                        gp.wait_ge(s_pool, npool[0])
                        gp.tensor_tensor(k_parts[:, 2, :], k_rest[:, :], k_parts[:, 1, :],
                                         ALU.subtract).then_inc(s_qk, 1)
                    if t == AOT - 6:
                        if b == 0:
                            gp.wait_ge(s_w_post, 16 * 10)
                        gp.wait_ge(s_x[b], 16)
                        if b >= 1:
                            gp.wait_ge(s_var, VAR_AT[0, b - 1] + 1)
                        for i in range(TT):
                            gp.tensor_tensor(x_bo[:, i, :], x_in[b][:, i, :], bo_sb[:, :],
                                             ALU.add).then_inc(s_xbo, 1)
                    for k, at in ((0, LN1), (1, LN2), (2, LN3), (3, LN4)):
                        if t == at + 1:
                            power(k, VAR_AT[k, b] + 1)
                    if t == WKV + 5:
                        gp.wait_ge(s_wgt, 2 * b + 2)
                        gp.wait_ge(s_act, A_COPIES["ctx", b] + 1)
                        if b >= 1:
                            gp.wait_ge(s_y, b)
                        gp.tensor_tensor(new_v[:, 0], wgt[:, 1], ctx_t[b % 3][:, :, :], ALU.mult).then_inc(s_pool, 1)
                        gp.tensor_tensor(new_v[:, 1], wgt[:, 3], ctx_t[b % 3][:, :, :], ALU.mult).then_inc(s_newv, 1)
                        npool[0] += 1
                    if t == WKV + 9:
                        gp.wait_ge(s_state, b + 1)
                        own(gp.tensor_tensor(y_old[:], wgt[:, 2], num[:, :, 0:T], ALU.mult))
                        gp.tensor_tensor(y_num[:], y_old[:], new_v[:, 1], ALU.add).then_inc(s_ynum, 1)
                    if t == X2T:
                        gp.wait_ge(s_x2, b + 1)
                        if b >= 1:
                            gp.wait_ge(s_var, VAR_AT[3, b - 1] + 1)
                        for i in range(TT):
                            gp.tensor_tensor(x2_beta[:, i, :], x2[b % 2][:, i, :], beta_sb[:, :],
                                             ALU.add).then_inc(s_x2b, 1)
                    if UP < t <= UP + NI and (t - UP) % 2 == 1:
                        m = (t - UP) // 2
                        n = NI // 2 * b + m
                        gp.wait_ge(s_relu, n + 1)
                        if m == 0 and b >= 1:
                            gp.wait_ge(s_b, B_DOWN[b - 1] + 1)
                        gp.tensor_tensor(inner_t[:, 2 * m:2 * m + 2, :], relu_t[n % 2][:, :, :],
                                         relu_t[n % 2][:, :, :], ALU.mult).then_inc(s_inner, 1)

        @block.vector
        def _(dve):
            nvec = [0]

            def own(ins):
                ins.then_inc(s_vec, 1)
                nvec[0] += 1

            def settle():
                dve.wait_ge(s_vec, nvec[0])

            def variance(k, src):
                settle()
                for i in range(TT):
                    own(nc.vector.bn_stats(stats[k][:, i, :], src[:, i, :]))
                settle()
                for i in range(TT):
                    own(nc.vector.bn_aggr(mean_var[k][:, i, :], stats[k][:, i, :]))
                settle()
                nc.vector.tensor_scalar(var_eps[k][:], mean_var[k][:, :, 1], EPS, None,
                                        ALU.add).then_inc(s_var, 1)

            def normalise(k, b, src, dst, done):
                dve.wait_ge(s_rstd, VAR_AT[k, b] + 1)
                for i in range(TT):
                    ins = nc.vector.tensor_scalar(dst[:, i, :], src[:, i, :], mean_var[k][:, i, 0:1],
                                                  rstd[k][:, i:i + 1], ALU.subtract, ALU.mult)
                    if i < TT - 1:
                        own(ins)
                        settle()
                ins.then_inc(done, 1)

            dve.wait_ge(s_w_att, 16 * 7)
            for c in range(CT):
                nc.vector.tensor_copy(wq_cols[:, c, :].rearrange("p (g d h) -> p g h d", g=NSET, d=HD),
                                      wq_sb[:, c, :].rearrange("p (g h d) -> p g h d", g=NSET, d=HD)) \
                    .then_inc(s_wcols, 1)
                nc.vector.tensor_copy(wk_cols[:, c, :].rearrange("p (d h) -> p h d", d=HD),
                                      wk_sb[:, c, :].rearrange("p (h d) -> p h d", d=HD)).then_inc(s_wcols, 1)

            for tick in TICKS:
                for b in range(B):
                    t = tick - b * PERIOD
                    if t == QP:
                        dve.wait_ge(s_qk1, 3 * b + 2)
                        if b >= 1:
                            dve.wait_ge(s_qk, b)
                        for g in range(NSET):
                            ins = nc.vector.scalar_tensor_tensor(q_rest[:, g, :], ps_a[:, g * T:g * T + T],
                                                                 bq_sb[:, g:g + 1], q_parts[:, g, 0, :],
                                                                 ALU.add, ALU.subtract)
                            ins.then_inc(s_rest, 1)
                        dve.wait_ge(s_rest, 3 * b + 2)
                        dve.sem_inc(s_a_free, 1)
                    if t == KV:
                        dve.wait_ge(s_qk1, 3 * b + 3)
                        nc.vector.scalar_tensor_tensor(k_rest[:, :], ps_a[0:KVD, 0:T], bk_sb[:, 0:1],
                                                       k_parts[:, 0, :], ALU.add, ALU.subtract).then_inc(s_rest, 1)
                        if b < 3:
                            dve.wait_ge(s_const, 9)
                        else:
                            dve.wait_ge(s_pv, 4 * NSET * (b - 2))
                        nc.vector.tensor_tensor(
                            v_cols[b % 3][:, :, :, 0:HD],
                            ps_a[:, T:T + TT * KVD].rearrange("p (i g d) -> p i g d", i=TT, d=HD),
                            bv_sb[:, :].rearrange("p (i g d) -> p i g d", i=1, d=HD).broadcast_to([P, TT, NG, HD]),
                            ALU.add).then_inc(s_v, 1)
                        dve.wait_ge(s_v, b + 1)
                        dve.wait_ge(s_rest, 3 * b + 3)
                        dve.sem_inc(s_a_free, 1)
                    for g in range(NSET):
                        s = NSET * b + g
                        i = t - MAXIMA - g * UNITS
                        if 0 <= i < UNITS:
                            n = UNITS * s + i
                            j, qt, half = i // 4, (i // 2) % 2, i % 2
                            dve.wait_ge(s_max_mm, n + 1)
                            h = REP * j + 2 * half
                            nc.vector.tensor_reduce(neg_max[s % 2][:, qt, h:h + 2], ps_max[n % 2][:, :, :], AX,
                                                    ALU.max, negate=True).then_inc(s_max, 1)
                        if i == UNITS - 1:
                            dve.wait_ge(s_max, UNITS * (s + 1))
                            if s >= 1:
                                dve.wait_ge(s_a, A_USE["m", (s - 1) // NSET, (s - 1) % NSET] + 1)
                            own(nc.vector.tensor_copy(max_parts[:, :, 0, :], neg_max[s % 2][:, :, :]))
                            settle()
                            own(nc.vector.tensor_tensor(max_rest[:], neg_max[s % 2][:, :, :],
                                                        max_parts[:, :, 0, :], ALU.subtract))
                            settle()
                            own(nc.vector.tensor_copy(max_parts[:, :, 1, :], max_rest[:]))
                            settle()
                            nc.vector.tensor_tensor(max_parts[:, :, 2, :], max_rest[:], max_parts[:, :, 1, :],
                                                    ALU.subtract).then_inc(s_mparts, 1)
                        if t == MROWS + g * UNITS:
                            dve.wait_ge(s_a, A_USE["m", b, g] + 1)
                            if s >= 1:
                                dve.wait_ge(s_mrows[(s - 1) % 3], 16 * ((s - 1) // 3 + 1))
                            nc.vector.tensor_copy(max_t[:, :], ps_a_bf[0:PARTS * HS, 0:T]).then_inc(s_maxt, 1)
                            dve.wait_ge(s_maxt, s + 1)
                            dve.sem_inc(s_a_free, 1)
                        for pair in range(2):
                            if t == heads_tick(g, pair):
                                dve.wait_ge(s_a, A_USE["heads", b, 2 * g + pair] + 1)
                                if g == 0 and pair == 0 and b >= 1:
                                    dve.wait_ge(s_a, A_USE["att", b - 1, 0] + 1)
                                view = ps_a[:, :].rearrange("p (r i j d) -> p r i j d", r=2, i=TT, d=32)
                                own(nc.vector.reciprocal(inv_sum[pair][:].rearrange("p r i j -> p (r i j)"),
                                                         ps_a[:, :].rearrange("p (x d) -> p x d", d=32)[:, :, HD]))
                                settle()
                                for i in range(TT):
                                    dst = att[:, i, (GS * g) * REP * HD:(GS * g + GS) * REP * HD] \
                                        .rearrange("p (j r d) -> p r j d", j=GS, r=REP)[:, 2 * pair:2 * pair + 2]
                                    ins = nc.vector.tensor_tensor(
                                        dst, view[:, :, i, :, 0:HD],
                                        inv_sum[pair][:, :, i, :].rearrange("p r (j d) -> p r j d", d=1)
                                        .broadcast_to([P, 2, GS, HD]), ALU.mult)
                                    if i < TT - 1:
                                        own(ins)
                                        settle()
                                ins.then_inc(s_att, 1)
                                dve.wait_ge(s_att, 2 * s + pair + 1)
                                dve.sem_inc(s_a_free, 1)
                    if t == LN1:
                        dve.wait_ge(s_a, A_USE["op", b, 0] + 1)
                        dve.wait_ge(s_xbo, TT * (b + 1))
                        own(nc.vector.tensor_tensor(flat(h1[:, :, :]), ps_a[:, :], flat(x_bo[:, :, :]), ALU.add))
                        settle()
                        dve.sem_inc(s_a_free, 1)
                        variance(0, h1)
                    if t == LN1 + 2:
                        normalise(0, b, h1, x1, s_x1)
                    if t == WKV:
                        dve.wait_ge(s_act, A_COPIES["x1", b] + 1)
                        if b == 0:
                            dve.wait_ge(s_w_post, 16 * 10)
                            dve.wait_ge(s_const, 9)
                        for c in range(CT):
                            own(nc.vector.tensor_tensor_scan(top[:, c, 1:T + 1],
                                                             decay_sb[:, c:c + 1].broadcast_to([P, T]),
                                                             x1_t[:, c, :], NEG, ALU.add, ALU.max))
                    if t == WKV + 1:
                        settle()
                        if b >= 1:
                            dve.wait_ge(s_wgt, 2 * b)
                        for c in range(CT):
                            own(nc.vector.scalar_tensor_tensor(arg[:, 0, c, :], top[:, c, 0:T], decay_sb[:, c:c + 1],
                                                               top[:, c, 1:T + 1], ALU.add, ALU.subtract))
                        settle()
                        nc.vector.tensor_tensor(arg[:, 1], x1_t[:, :, :], top[:, :, 1:T + 1],
                                                ALU.subtract).then_inc(s_arg, 1)
                    if t == WKV + 2:
                        for c in range(CT):
                            own(nc.vector.scalar_tensor_tensor(gap[:, c, :], x1_t[:, c, :], bonus_sb[:, c:c + 1],
                                                               top[:, c, 0:T], ALU.add, ALU.subtract))
                        settle()
                        own(nc.vector.tensor_scalar(arg[:, 2], gap[:], 0.0, -1.0, ALU.max, ALU.mult))
                        settle()
                        nc.vector.tensor_scalar(arg[:, 3], gap[:], 0.0, None, ALU.min).then_inc(s_arg, 1)
                    if t == WKV + 6:
                        dve.wait_ge(s_wgt, 2 * b + 1)
                        for c in range(CT):
                            own(nc.vector.tensor_tensor_scan(den[:, c, 1:T + 1], wgt[:, 0, c, :], wgt[:, 1, c, :],
                                                             0.0, ALU.mult, ALU.add))
                    if t == WKV + 7:
                        dve.wait_ge(s_newv, b + 1)
                        settle()
                        for c in range(CT):
                            ins = nc.vector.tensor_tensor_scan(num[:, c, 1:T + 1], wgt[:, 0, c, :],
                                                               new_v[:, 0, c, :], 0.0, ALU.mult, ALU.add)
                            if c < CT - 1:
                                own(ins)
                                settle()
                        ins.then_inc(s_state, 1)
                    if t == WKV + 8:
                        own(nc.vector.tensor_tensor(y_den[:], wgt[:, 2], den[:, :, 0:T], ALU.mult))
                        settle()
                        own(nc.vector.tensor_tensor(y_den[:], y_den[:], wgt[:, 3], ALU.add))
                    if t == WKV + 9:
                        settle()
                        own(nc.vector.reciprocal(flat(y_inv[:, :, :]), flat(y_den[:, :, :])))
                    if t == WKV + 12:
                        dve.wait_ge(s_ynum, b + 1)
                        settle()
                        nc.vector.tensor_tensor(y_t[:], y_num[:], y_inv[:], ALU.mult).then_inc(s_y, 1)
                    if t == LN2:
                        dve.wait_ge(s_a, A_USE["y", b, 0] + 1)
                        own(nc.vector.tensor_tensor(flat(h2[:, :, :]), ps_a[:, :], flat(x1[:, :, :]), ALU.add))
                        settle()
                        dve.sem_inc(s_a_free, 1)
                        variance(1, h2)
                    if t == LN2 + 2:
                        normalise(1, b, h2, x2[b % 2], s_x2)
                    if t == GATE + 1:
                        dve.wait_ge(s_a, A_USE["gate", b, 0] + 1)
                        for i in range(TT):
                            own(nc.vector.max(top8[:, i, :], ps_a[:, i * NE:i * NE + NE]))
                        settle()
                        dve.sem_inc(s_a_free, 1)
                        if b >= 1:
                            dve.wait_ge(s_eout, TT * b)
                        nc.vector.tensor_tensor(route[:], top8[:, :, 0], top8[:, :, 1], ALU.add).then_inc(s_route, 1)
                    if t == LN3:
                        dve.wait_ge(s_b, B_DOWN[b] + 1)
                        dve.wait_ge(s_eout, TT * (b + 1))
                        own(nc.vector.tensor_tensor(flat(h3[:, :, :]), ps_b[:, :], flat(expert_out[:, :, :]), ALU.add))
                        settle()
                        dve.sem_inc(s_b_free, 1)
                        variance(2, h3)
                    if t == LN3 + 1:
                        for i in range(TT):
                            own(nc.vector.scalar_tensor_tensor(h3g[:, i, :], h3[:, i, :], mean_var[2][:, i, 0:1],
                                                               gamma_sb[:, :], ALU.subtract, ALU.mult))
                    if t == LN4:
                        dve.wait_ge(s_rstd, VAR_AT[2, b] + 1)
                        dve.wait_ge(s_x2b, TT * (b + 1))
                        settle()
                        for i in range(TT):
                            own(nc.vector.scalar_tensor_tensor(h4[:, i, :], h3g[:, i, :], rstd[2][:, i:i + 1],
                                                               x2_beta[:, i, :], ALU.mult, ALU.add))
                        variance(3, h4)
                    if t == LN4 + 2:
                        if b >= 1:
                            dve.wait_ge(s_store, 16 * b)
                        normalise(3, b, h4, y_out, s_out)


INPUTS = ["x", "ctx_2048", "L0_attn_Wq", "L0_attn_bq", "L0_attn_Wk", "L0_attn_bk", "L0_attn_Wv", "L0_attn_bv",
          "L0_attn_Wo", "L0_attn_bo", "L0_xattn_w", "L0_xattn_u", "L0_ffn_gate_w", "L0_ffn_up_w",
          "L0_ffn_down_w", "L0_ffn_expert_weight", "L0_ffn_ln_gamma", "L0_ffn_ln_beta"]


def kernel(**inputs):
    import concourse.bacc as bacc
    from concourse.bass_utils import run_bass_kernel_spmd

    nc = bacc.Bacc("TRN2", target_bir_lowering=False, num_devices=1)
    arrays, args = {}, []
    for name in INPUTS:
        a = np.ascontiguousarray(inputs[name])
        arrays[f"in_{name}"] = a
        args.append(nc.dram_tensor(f"in_{name}", a.shape, mybir.dt.from_np(a.dtype), kind="ExternalInput").ap())
    shape = arrays["in_x"].shape
    args.append(nc.dram_tensor("out_y", shape, mybir.dt.float32, kind="ExternalOutput").ap())
    decoder_layer(nc, *args)
    r = run_bass_kernel_spmd(nc, [arrays], core_ids=[0])
    return r.results[0]["out_y"]
```

```python
import concourse.bass as bass
from concourse import mybir
from contextlib import ExitStack
import numpy as np


def decoder_layer(nc, x, ctx, wq, bq, wk, bk, wv, bv, wo, bo, w_decay, u_bonus,
                  gate_w, up_w, down_w, expert_w, ln_gamma, ln_beta, out):
    fp32, bf16 = mybir.dt.float32, mybir.dt.bfloat16
    ALU = mybir.AluOpType
    ACT = mybir.ActivationFunctionType
    AX = mybir.AxisListType.X

    B, T, D = x.shape
    P = 128
    TT = T // P
    CT = D // P
    KVD = wk.shape[1]
    HD = 8
    NG = KVD // HD
    REP = D // KVD
    GS = 4
    NSET = NG // GS
    HS = GS * REP
    PARTS = 3
    BLOCKS = [(0, 0), (1, 0), (0, 1), (1, 1), (2, 0), (0, 2)]
    QK = len(BLOCKS) * HD
    QKP = 96
    QKM = QKP + PARTS
    SCALE = float(np.float32(1.0) / np.sqrt(np.float32(HD)))
    NI = up_w.shape[1] // P
    NE = gate_w.shape[1]
    EPS = 1e-5
    NEG = -1e38
    UNITS = 16
    W2 = TT * D

    PERIOD = NSET * UNITS
    XT, KV, QP = -37, -33, -31
    ROWS = (-24, -10)
    CTXT = -25
    MAXIMA = -UNITS
    MROWS = 2
    EXP = 7
    PV_LAG = 2
    AOT, OP, LN1 = 46, 47, 49
    X1T = 54
    WKV = 55
    YT = 76
    LN2 = 77
    X2T, EXPERT, UP = 82, 83, 89
    DOWN = 98
    LN3, LN4 = 104, 107
    STORE = 114
    LATE = [-1, -1, 2, -3]
    TICKS = range(XT, (B - 1) * PERIOD + STORE + 1)

    ectx = ExitStack()
    with ectx:
        def sb(name, shape, dt=fp32):
            return ectx.enter_context(nc.sbuf_tensor(name, shape, dt))

        def ps(name, shape, dt=fp32):
            return ectx.enter_context(nc.psum_tensor(name, shape, dt))

        def sem(name):
            return ectx.enter_context(nc.semaphore(name))

        wq_sb = sb("wq_sb", [P, CT, D])
        wk_sb = sb("wk_sb", [P, CT, KVD])
        wq_cols = sb("wq_cols", [P, CT, D])
        wk_cols = sb("wk_cols", [P, CT, KVD])
        wv_sb = sb("wv_sb", [P, CT, KVD])
        wo_sb = sb("wo_sb", [P, CT, D])
        up_sb = sb("up_sb", [P, CT, NI * P])
        down_sb = sb("down_sb", [P, NI, D])
        expert_sb = sb("expert_sb", [P, CT, D + NE])
        bq_sb = sb("bq_sb", [P, NSET])
        bk_sb = sb("bk_sb", [KVD, 1])
        bv_sb = sb("bv_sb", [P, KVD])
        bo_sb = sb("bo_sb", [P, D])
        decay_sb = sb("decay_sb", [P, CT])
        bonus_sb = sb("bonus_sb", [P, CT])
        gamma_sb = sb("gamma_sb", [P, D])
        beta_sb = sb("beta_sb", [P, D])
        ident = sb("ident", [P, P])
        ident_bf = sb("ident_bf", [P, P], bf16)
        minus_half = sb("minus_half", [P, TT])

        x_in = [sb(f"x_in{b}", [P, TT, D]) for b in range(B)]
        ctx_in = [sb(f"ctx_in{b}", [P, TT, D]) for b in range(B)]
        x_t = sb("x_t", [P, CT, T])
        ctx_t = [sb(f"ctx_t{i}", [P, CT, T]) for i in range(3)]
        q_parts = sb("q_parts", [P, NSET, PARTS, T], bf16)
        q_rest = sb("q_rest", [P, NSET, T])
        k_parts = sb("k_parts", [KVD, PARTS, T], bf16)
        k_rest = sb("k_rest", [KVD, T])
        q_rows = [sb(f"q_rows{i}", [P, HS, T], bf16) for i in range(3)]
        k_rows = [sb(f"k_rows{i}", [P, NG, T], bf16) for i in range(2)]
        v_cols = [sb(f"v_cols{i}", [P, TT, NG, 32]) for i in range(3)]
        neg_max = [sb(f"neg_max{i}", [P, TT, HS]) for i in range(2)]
        max_rest = sb("max_rest", [P, TT, HS])
        max_parts = sb("max_parts", [P, TT, PARTS, HS], bf16)
        max_t = sb("max_t", [PARTS * HS, T], bf16)
        probs = [sb(f"probs{i}", [P, 2 * T]) for i in range(8)]
        heads_t = [sb(f"heads_t{i}", [P, 2 * T]) for i in range(2)]
        inv_sum = [sb(f"inv_sum{i}", [P, 2, TT, GS]) for i in range(2)]
        att = sb("att", [P, TT, D])
        att_t = sb("att_t", [P, CT, T])
        x_bo = sb("x_bo", [P, TT, D])
        h1 = sb("h1", [P, TT, D])
        x1 = sb("x1", [P, TT, D])
        x1_t = sb("x1_t", [P, CT, T])
        top = sb("top", [P, CT, T + 1])
        num = sb("num", [P, CT, T + 1])
        den = sb("den", [P, CT, T + 1])
        arg = sb("arg", [P, 4, CT, T])
        wgt = sb("wgt", [P, 4, CT, T])
        gap = sb("gap", [P, CT, T])
        new_v = sb("new_v", [P, 2, CT, T])
        y_num = sb("y_num", [P, CT, T])
        y_old = sb("y_old", [P, CT, T])
        y_den = sb("y_den", [P, CT, T])
        y_inv = sb("y_inv", [P, CT, T])
        y_t = sb("y_t", [P, CT, T])
        h2 = sb("h2", [P, TT, D])
        x2 = [sb(f"x2_{i}", [P, TT, D]) for i in range(2)]
        x2_beta = sb("x2_beta", [P, TT, D])
        x2_t = sb("x2_t", [P, CT, T])
        top8 = sb("top8", [P, TT, 8])
        route = sb("route", [P, TT])
        expert_out = sb("expert_out", [P, TT, D])
        relu_t = [sb(f"relu_t{i}", [P, 2, T]) for i in range(2)]
        inner_t = sb("inner_t", [P, NI, T])
        h3 = sb("h3", [P, TT, D])
        h3g = sb("h3g", [P, TT, D])
        h4 = sb("h4", [P, TT, D])
        y_out = sb("y_out", [P, TT, D])
        stats = [sb(f"stats{i}", [P, TT, 6]) for i in range(4)]
        mean_var = [sb(f"mean_var{i}", [P, TT, 2]) for i in range(4)]
        var_eps = [sb(f"var_eps{i}", [P, TT]) for i in range(4)]
        rstd = [sb(f"rstd{i}", [P, TT]) for i in range(4)]

        ps_max = [ps(f"ps_max{i}", [P, 2, T]) for i in range(2)]
        ps_exp = [ps(f"ps_exp{i}", [P, 2 * T]) for i in range(2)]
        ps_heads = [ps(f"ps_heads{i}", [P, 2 * T]) for i in range(2)]
        ps_a = ps("ps_a", [P, 2 * T])
        ps_b = ps("ps_b", [P, 2 * T])
        ps_a_bf = ps_a[:, 0:T].bitcast(bf16)

        s_wqk = sem("s_wqk")
        s_wv = sem("s_wv")
        s_bias = sem("s_bias")
        s_wcols = sem("s_wcols")
        s_w_post = sem("s_w_post")
        s_x = [sem(f"s_x_in{b}") for b in range(B)]
        s_ctx = [sem(f"s_ctx_in{b}") for b in range(B)]
        s_ident = sem("s_ident")
        s_zero = sem("s_zero")
        s_ones = sem("s_ones")
        s_const = sem("s_const")
        s_a = sem("s_a")
        s_a_read = sem("s_a_read")
        s_b = sem("s_b")
        s_b_read = sem("s_b_read")
        s_k1, s_q1 = sem("s_k1"), sem("s_q1")
        s_k2, s_q2 = sem("s_k2"), sem("s_q2")
        s_k3, s_q3 = sem("s_k3"), sem("s_q3")
        s_v = sem("s_v")
        s_rows = [sem(f"s_rows{i}") for i in range(3)]
        s_krows = [sem(f"s_krows{i}") for i in range(2)]
        s_max_mm = sem("s_max_mm")
        s_max = sem("s_max")
        s_mparts = sem("s_mparts")
        s_mrows = [sem(f"s_mrows{i}") for i in range(3)]
        s_exp_mm = sem("s_exp_mm")
        s_exp = sem("s_exp")
        s_pv = sem("s_pv")
        s_heads = sem("s_heads")
        s_headst = sem("s_headst")
        s_att = sem("s_att")
        s_xbo = sem("s_xbo")
        s_var = sem("s_var")
        s_rstd = sem("s_rstd")
        s_x1 = sem("s_x1")
        s_arg = sem("s_arg")
        s_wgt = sem("s_wgt")
        s_newv = sem("s_newv")
        s_state = sem("s_state")
        s_ynum = sem("s_ynum")
        s_y = sem("s_y")
        s_x2 = sem("s_x2")
        s_x2b = sem("s_x2b")
        s_route = sem("s_route")
        s_inner = sem("s_inner")
        s_out = sem("s_out")
        s_store = sem("s_store")
        s_vec = sem("s_vec")
        s_pool = sem("s_pool")

        def flat(ap):
            return ap.rearrange("p a b -> p (a b)")

        def row(ap):
            return ap.rearrange("(a n) -> a n", a=1)

        def in_order(steps):
            order = [(name, b) for tick in TICKS for b in range(B) for name, at in steps
                     if tick - b * PERIOD - (LATE[b] if at >= YT else 0) == at]
            return {step: i for i, step in enumerate(order)}

        A_USE = in_order((("x", XT), ("q", QP), ("kv", KV), ("ctx", CTXT), ("m0", MROWS), ("m1", MROWS + UNITS),
                          ("att", AOT), ("op", OP), ("x1", X1T), ("y", YT), ("x2", X2T)))
        B_USE = in_order((("expert0", EXPERT), ("expert1", EXPERT + 2), *((f"up{i}", UP + i) for i in range(0, NI, 2)),
                          ("down", DOWN)))
        LN_USE = in_order(((0, LN1), (1, LN2), (2, LN3), (3, LN4)))

        def heads_out(g, pair):
            return EXP + g * UNITS + 8 * pair + 8 + PV_LAG

        def up_bank(b, late):
            return ps_exp[1] if b == B - 1 and (late - UP) % 4 == 2 else ps_b

        block = ectx.enter_context(nc.Block())

        @block.sync
        def _(sp):
            def token_tiles(a):
                return a.rearrange("(t p) c -> p t c", p=P)

            sp.dma_start(x_in[0][:], token_tiles(x[0])).then_inc(s_x[0], 16)
            sp.dma_start(wk_sb[:], token_tiles(wk)).then_inc(s_wqk, 16)
            sp.dma_start(wq_sb[:], token_tiles(wq)).then_inc(s_wqk, 16)
            sp.dma_start(wv_sb[:], token_tiles(wv)).then_inc(s_wv, 16)
            sp.dma_start(bk_sb[:], bk.rearrange("(h d) -> d h", d=HD),
                         allow_slow_non_contiguous=True).then_inc(s_bias, 16)
            for g in range(NSET):
                sp.dma_start(bq_sb[:, g:g + 1], bq[g * P:g * P + P].rearrange("(h d) -> d h", d=HD),
                             allow_slow_non_contiguous=True).then_inc(s_bias, 16)
            sp.dma_start(bv_sb[:], row(bv).broadcast_to([P, KVD])).then_inc(s_bias, 16)
            for b in range(1, B):
                sp.dma_start(x_in[b][:], token_tiles(x[b])).then_inc(s_x[b], 16)
            for b in range(B):
                sp.dma_start(ctx_in[b][:], token_tiles(ctx[b])).then_inc(s_ctx[b], 16)
            for dst, src in ((wo_sb[:], wo), (up_sb[:], up_w), (down_sb[:], down_w),
                             (expert_sb[:, :, 0:D], expert_w), (expert_sb[:, :, D:D + NE], gate_w)):
                sp.dma_start(dst, token_tiles(src)).then_inc(s_w_post, 16)
            for dst, src in ((bo_sb, bo), (gamma_sb, ln_gamma), (beta_sb, ln_beta)):
                sp.dma_start(dst[:], row(src).broadcast_to([P, D])).then_inc(s_w_post, 16)
            for dst, src in ((decay_sb, w_decay), (bonus_sb, u_bonus)):
                sp.dma_start(dst[:], src.rearrange("(c p) -> p c", p=P),
                             allow_slow_non_contiguous=True).then_inc(s_w_post, 16)

            def rows_of_set(b, g):
                s = NSET * b + g
                if g == 0:
                    sp.wait_ge(s_ones, min(b, 1) + 1)
                    sp.wait_ge(s_k3, b + 1)
                    if b >= 2:
                        sp.wait_ge(s_exp_mm, UNITS * NSET * (b - 1))
                    for r, (_, kp) in enumerate(BLOCKS):
                        sp.dma_start(k_rows[b % 2][HD * r:HD * r + HD, :, :],
                                     k_parts[:, kp, :]).then_inc(s_krows[b % 2], 16)
                sp.wait_ge(s_q3, b + 1)
                sp.wait_ge(s_zero, min(s, 2) + 1)
                if s >= 3:
                    sp.wait_ge(s_exp_mm, UNITS * (s - 2))
                for r, (qp, _) in enumerate(BLOCKS):
                    sp.dma_start(q_rows[s % 3][HD * r:HD * r + HD, :, :],
                                 q_parts[:, g, qp, :]).then_inc(s_rows[s % 3], 16)

            for tick in TICKS:
                for b in range(B):
                    t = tick - b * PERIOD
                    late = t - LATE[b]
                    for g in range(NSET):
                        if t == ROWS[g]:
                            rows_of_set(b, g)
                        if t == MROWS + g * UNITS + 1:
                            s = NSET * b + g
                            sp.wait_ge(s_a_read, A_USE[f"m{g}", b] + 1)
                            sp.dma_start(q_rows[s % 3][QKP:QKM, :, :],
                                         max_t[:, :]).then_inc(s_mrows[s % 3], 16)
                    if late == STORE:
                        sp.wait_ge(s_out, b + 1)
                        sp.dma_start(token_tiles(out[b]), y_out[:]).then_inc(s_store, 16)
            sp.wait_ge(s_store, 16 * B)

        @block.tensor
        def _(pe):
            ps_a_tiles = ps_a[:, :].rearrange("p (c t) -> p c t", c=CT)

            def open_a(use):
                if A_USE[use] >= 1:
                    pe.wait_ge(s_a_read, A_USE[use])

            def open_b(use):
                if B_USE[use] >= 1:
                    pe.wait_ge(s_b_read, B_USE[use])

            def transposes(src):
                for c in range(CT):
                    for i in range(TT):
                        last = nc.tensor.transpose(ps_a[:, c * T + i * P:c * T + i * P + P],
                                                   src[:, i, c * P:c * P + P], ident[:, :])
                last.then_inc(s_a, 1)

            def maxima_unit(b, g, i):
                s, n = NSET * b + g, UNITS * (NSET * b + g) + i
                j, qt, half = i // 4, (i // 2) % 2, i % 2
                if i == 0:
                    pe.wait_ge(s_rows[s % 3], 16 * len(BLOCKS) * (s // 3 + 1))
                    if g == 0:
                        pe.wait_ge(s_krows[b % 2], 16 * len(BLOCKS) * (b // 2 + 1))
                if n >= 2:
                    pe.wait_ge(s_max, n - 1)
                for r in range(2):
                    last = nc.tensor.matmul(ps_max[n % 2][:, r, :],
                                            q_rows[s % 3][0:QKP, REP * j + 2 * half + r, qt * P:qt * P + P],
                                            k_rows[b % 2][0:QKP, GS * g + j, :], start=True, stop=True)
                last.then_inc(s_max_mm, 1)

            def exp_unit(b, g, i):
                s, n = NSET * b + g, UNITS * (NSET * b + g) + i
                pair, kt, j = i // 8, (i // 4) % 2, i % 4
                if i == 0:
                    pe.wait_ge(s_mrows[s % 3], 16 * (s // 3 + 1))
                if n >= 2:
                    pe.wait_ge(s_exp, n - 1)
                nc.tensor.matmul(ps_exp[n % 2][:, :], k_rows[b % 2][0:QKM, GS * g + j, kt * P:kt * P + P],
                                 q_rows[s % 3][0:QKM, REP * j + 2 * pair:REP * j + 2 * pair + 2, :]
                                 .rearrange("p h t -> p (h t)"), start=True, stop=True).then_inc(s_exp_mm, 1)

            def pv_group(b, g, i):
                s, n = NSET * b + g, 4 * (NSET * b + g) + i
                pair, kt = i // 2, i % 2
                if i == 0 and g == 0:
                    pe.wait_ge(s_v, b + 1)
                pe.wait_ge(s_exp, 4 * n + 4)
                if kt == 0 and s >= 1:
                    pe.wait_ge(s_att, 2 * (s - 1) + pair + 1)
                for j in range(GS):
                    last = nc.tensor.matmul(ps_heads[pair][32 * j:32 * j + 32, :],
                                            v_cols[b % 3][:, kt, GS * g + j, :], probs[(4 * n + j) % 8][:, :],
                                            start=(kt == 0), stop=(kt == 1))
                last.then_inc(s_pv, 1)

            pe.wait_ge(s_ident, 2)
            for tick in TICKS:
                for b in range(B):
                    for g in range(NSET):
                        i = tick - b * PERIOD - EXP - g * UNITS
                        if 0 <= i < UNITS:
                            exp_unit(b, g, i)
                for b in range(B):
                    for g in range(NSET):
                        i = tick - b * PERIOD - MAXIMA - g * UNITS
                        if 0 <= i < UNITS:
                            maxima_unit(b, g, i)
                for b in range(B):
                    t = tick - b * PERIOD
                    late = t - LATE[b]
                    if t == XT:
                        pe.wait_ge(s_x[b], 16)
                        open_a(("x", b))
                        transposes(x_in[b])
                    if t == KV:
                        if b == 0:
                            pe.wait_ge(s_wcols, 2 * CT)
                            pe.wait_ge(s_wv, 16)
                        open_a(("kv", b))
                        pe.wait_ge(s_a_read, A_USE["x", b] + 1)
                        for c in range(CT):
                            nc.tensor.matmul(ps_a[0:KVD, 0:T], wk_cols[:, c, :], x_t[:, c, :],
                                             start=(c == 0), stop=(c == CT - 1))
                        for i in range(TT):
                            for c in range(CT):
                                last = nc.tensor.matmul(ps_a[:, T + i * KVD:T + i * KVD + KVD],
                                                        x_t[:, c, i * P:i * P + P], wv_sb[:, c, :],
                                                        start=(c == 0), stop=(c == CT - 1))
                        last.then_inc(s_a, 1)
                    if t == QP:
                        open_a(("q", b))
                        for g in range(NSET):
                            for c in range(CT):
                                last = nc.tensor.matmul(ps_a_tiles[:, g, :], wq_cols[:, c, g * P:g * P + P],
                                                        x_t[:, c, :], start=(c == 0), stop=(c == CT - 1))
                        last.then_inc(s_a, 1)
                    if t == CTXT:
                        pe.wait_ge(s_ctx[b], 16)
                        open_a(("ctx", b))
                        transposes(ctx_in[b])
                    for g in range(NSET):
                        if t == MROWS + g * UNITS:
                            s = NSET * b + g
                            open_a((f"m{g}", b))
                            pe.wait_ge(s_mparts, s + 1)
                            for i in range(TT):
                                last = nc.tensor.transpose(ps_a_bf[0:PARTS * HS, i * P:i * P + P],
                                                           max_parts[:, i, :, :].rearrange("p a b -> p (a b)"),
                                                           ident_bf[:, :])
                            last.then_inc(s_a, 1)
                    for g in range(NSET):
                        i = t - EXP - g * UNITS - 3 - PV_LAG
                        if i in (0, 4, 8, 12):
                            pv_group(b, g, i // 4)
                        for pair in range(2):
                            if t == heads_out(g, pair) + 2:
                                pe.wait_ge(s_heads, 2 * (NSET * b + g) + pair + 1)
                                for i in range(4):
                                    last = nc.tensor.transpose(ps_heads[pair][:, i * P:i * P + P],
                                                               heads_t[pair][:, i * P:i * P + P], ident[:, :])
                                last.then_inc(s_headst, 1)
                    if t == AOT:
                        open_a(("att", b))
                        pe.wait_ge(s_att, 2 * NSET * (b + 1))
                        transposes(att)
                    if t == OP:
                        if b == 0:
                            pe.wait_ge(s_w_post, 16 * 10)
                        open_a(("op", b))
                        pe.wait_ge(s_a_read, A_USE["att", b] + 1)
                        for i in range(TT):
                            for c in range(CT):
                                last = nc.tensor.matmul(ps_a[:, i * D:i * D + D], att_t[:, c, i * P:i * P + P],
                                                        wo_sb[:, c, :], start=(c == 0), stop=(c == CT - 1))
                        last.then_inc(s_a, 1)
                    if t == X1T:
                        open_a(("x1", b))
                        pe.wait_ge(s_x1, b + 1)
                        transposes(x1)
                    if late == YT:
                        open_a(("y", b))
                        pe.wait_ge(s_y, b + 1)
                        transposes(y_t)
                    if late == X2T:
                        open_a(("x2", b))
                        pe.wait_ge(s_x2, b + 1)
                        transposes(x2[b % 2])
                    if late in (EXPERT, EXPERT + 2):
                        i = (late - EXPERT) // 2
                        open_b((f"expert{i}", b))
                        pe.wait_ge(s_a_read, A_USE["x2", b] + 1)
                        for c in range(CT):
                            last = nc.tensor.matmul(ps_b[:, 0:D + NE], x2_t[:, c, i * P:i * P + P],
                                                    expert_sb[:, c, :], start=(c == 0), stop=(c == CT - 1))
                        last.then_inc(s_b, 1)
                    if UP <= late < UP + NI and (late - UP) % 2 == 0:
                        if b < B - 1 or late == UP:
                            open_b((f"up{late - UP}", b))
                        elif late > UP + 2:
                            pe.wait_ge(s_b_read, B_USE[f"up{late - UP - 4}", b] + 1)
                        for i in range(2):
                            for c in range(CT):
                                m = late - UP + i
                                last = nc.tensor.matmul(up_bank(b, late)[:, i * T:i * T + T], up_sb[:, c, m * P:m * P + P],
                                                        x2_t[:, c, :], start=(c == 0), stop=(c == CT - 1))
                        last.then_inc(s_b, 1)
                    if DOWN <= late < DOWN + 4:
                        i, half = (late - DOWN) // 2, (late - DOWN) % 2
                        if late == DOWN:
                            open_b(("down", b))
                        for m in range(half * NI // 2, (half + 1) * NI // 2):
                            if i == 0 and m % 2 == 0:
                                pe.wait_ge(s_inner, NI // 2 * b + m // 2 + 1)
                            last = nc.tensor.matmul(ps_b[:, i * D:i * D + D], inner_t[:, m, i * P:i * P + P],
                                                    down_sb[:, m, :], start=(m == 0), stop=(m == NI - 1))
                        if late == DOWN + 3:
                            last.then_inc(s_b, 1)

        @block.scalar
        def _(act):
            def evacuate(name, b, dst):
                act.wait_ge(s_a, A_USE[name, b] + 1)
                nc.scalar.activation(dst, ps_a[:, :], ACT.Copy).then_inc(s_a_read, 1)

            for tick in TICKS:
                for b in range(B):
                    for g in range(NSET):
                        i = tick - b * PERIOD - EXP - g * UNITS
                        if 0 <= i < UNITS:
                            n = UNITS * (NSET * b + g) + i
                            act.wait_ge(s_exp_mm, n + 1)
                            if n >= 8:
                                act.wait_ge(s_pv, (n - 8) // 4 + 1)
                            nc.scalar.activation(probs[n % 8][:, :], ps_exp[n % 2][:, :], ACT.Exp,
                                                 scale=SCALE).then_inc(s_exp, 1)
                for b in range(B):
                    t = tick - b * PERIOD
                    late = t - LATE[b]
                    if t == XT:
                        evacuate("x", b, flat(x_t[:, :, :]))
                    if t == KV:
                        act.wait_ge(s_a, A_USE["kv", b] + 1)
                        if b == 0:
                            act.wait_ge(s_bias, 16 * (NSET + 2))
                        if b >= 1:
                            act.wait_ge(s_krows[(b - 1) % 2], 16 * len(BLOCKS) * ((b - 1) // 2 + 1))
                        nc.scalar.activation(k_parts[:, 0, :], ps_a[0:KVD, 0:T], ACT.Identity,
                                             bias=bk_sb[:, 0:1]).then_inc(s_k1, 1)
                    if t == KV + 1:
                        act.wait_ge(s_a_read, A_USE["kv", b] + 1)
                        nc.scalar.activation(k_parts[:, 1, :], k_rest[:, :], ACT.Copy).then_inc(s_k2, 1)
                    if t == QP:
                        act.wait_ge(s_a, A_USE["q", b] + 1)
                        if b >= 1:
                            for s in (NSET * b - 1, NSET * b - 2):
                                act.wait_ge(s_rows[s % 3], 16 * len(BLOCKS) * (s // 3 + 1))
                        for g in range(NSET):
                            nc.scalar.activation(q_parts[:, g, 0, :], ps_a[:, g * T:g * T + T], ACT.Identity,
                                                 bias=bq_sb[:, g:g + 1]).then_inc(s_q1, 1)
                    if t == QP + 1:
                        act.wait_ge(s_a_read, A_USE["q", b] + 1)
                        nc.scalar.activation(q_parts[:, :, 1, :], q_rest[:, :, :], ACT.Copy).then_inc(s_q2, 1)
                    if t == CTXT:
                        if b >= 3:
                            act.wait_ge(s_newv, b - 2)
                        evacuate("ctx", b, flat(ctx_t[b % 3][:, :, :]))
                    for g in range(NSET):
                        for pair in range(2):
                            if t == heads_out(g, pair):
                                n = 2 * (NSET * b + g) + pair
                                act.wait_ge(s_pv, 2 * n + 2)
                                if n >= 2:
                                    act.wait_ge(s_headst, n - 1)
                                nc.scalar.activation(heads_t[pair][:, :], ps_heads[pair][:, :],
                                                     ACT.Copy).then_inc(s_heads, 1)
                    if t == AOT:
                        evacuate("att", b, flat(att_t[:, :, :]))
                    if t == X1T:
                        if b >= 1:
                            act.wait_ge(s_arg, 2 * b)
                        evacuate("x1", b, flat(x1_t[:, :, :]))
                    if t in (WKV + 3, WKV + 4):
                        half = t - WKV - 3
                        act.wait_ge(s_arg, 2 * b + half + 1)
                        if b >= 1:
                            act.wait_ge(s_y, b)
                        nc.scalar.activation(wgt[:, 2 * half:2 * half + 2].rearrange("p a c t -> p (a c t)"),
                                             arg[:, 2 * half:2 * half + 2].rearrange("p a c t -> p (a c t)"),
                                             ACT.Exp).then_inc(s_wgt, 1)
                    if late == X2T:
                        evacuate("x2", b, flat(x2_t[:, :, :]))
                    if late in (EXPERT, EXPERT + 2):
                        i = (late - EXPERT) // 2
                        act.wait_ge(s_route, TT * b + i + 1)
                        if i == 0 and b >= 1:
                            act.wait_ge(s_b_read, B_USE["down", b - 1] + 1)
                        nc.scalar.activation(expert_out[:, i, :], ps_b[:, 0:D], ACT.Copy,
                                             scale=route[:, i:i + 1]).then_inc(s_b_read, 1)
                    if UP <= late < UP + NI and (late - UP) % 2 == 0:
                        n = NI // 2 * b + (late - UP) // 2
                        act.wait_ge(s_b, B_USE[f"up{late - UP}", b] + 1)
                        if n >= 2:
                            act.wait_ge(s_inner, n - 1)
                        nc.scalar.activation(flat(relu_t[n % 2][:, :, :]), up_bank(b, late)[:, :], ACT.Relu).then_inc(s_b_read, 1)
                    if UP < late <= UP + NI and (late - UP) % 2 == 1:
                        m = (late - UP) // 2
                        n = NI // 2 * b + m
                        act.wait_ge(s_b_read, B_USE[f"up{2 * m}", b] + 1)
                        if m == 0 and b >= 1:
                            act.wait_ge(s_b, B_USE["down", b - 1] + 1)
                        nc.scalar.activation(flat(inner_t[:, 2 * m:2 * m + 2, :]), flat(relu_t[n % 2][:, :, :]),
                                             ACT.Square).then_inc(s_inner, 1)

        @block.gpsimd
        def _(gp):
            npool = [0]

            def own(ins):
                ins.then_inc(s_pool, 1)
                npool[0] += 1
                gp.wait_ge(s_pool, npool[0])

            own(gp.memset(ident[:], 0.0))
            gp.affine_select(out=ident[:], in_=ident[:], compare_op=ALU.not_equal, fill=1.0, base=0,
                             pattern=[[-1, P]], channel_multiplier=1).then_inc(s_ident, 1)
            gp.wait_ge(s_ident, 1)
            gp.tensor_copy(ident_bf[:], ident[:]).then_inc(s_ident, 1)
            for i in range(3):
                own(gp.memset(v_cols[i][:], 0.0))
                gp.memset(v_cols[i][:, :, :, HD:HD + 1], 1.0).then_inc(s_const, 1)
            gp.memset(minus_half[:], -0.5).then_inc(s_const, 1)
            gp.memset(top[:, :, 0:1], NEG).then_inc(s_const, 1)
            gp.memset(num[:, :, 0:1], 0.0).then_inc(s_const, 1)
            gp.memset(den[:, :, 0:1], 0.0).then_inc(s_const, 1)
            for i in range(3):
                if i < 2:
                    gp.memset(k_rows[i][:], 1.0).then_inc(s_ones, 1)
                gp.memset(q_rows[i][:].rearrange("p h t -> p (h t)").bitcast(fp32), 0.0).then_inc(s_zero, 1)
            gp.wait_ge(s_const, 7)

            def power(k, n):
                gp.wait_ge(s_var, n)
                gp.tensor_tensor(rstd[k][:], var_eps[k][:], minus_half[:], ALU.pow).then_inc(s_rstd, 1)

            for tick in TICKS:
                for b in range(B):
                    t = tick - b * PERIOD
                    late = t - LATE[b]
                    if t == AOT - 6:
                        if b == 0:
                            gp.wait_ge(s_w_post, 16 * 10)
                        gp.wait_ge(s_x[b], 16)
                        if b >= 1:
                            gp.wait_ge(s_var, LN_USE[0, b - 1] + 1)
                        for i in range(TT):
                            gp.tensor_tensor(x_bo[:, i, :], x_in[b][:, i, :], bo_sb[:, :],
                                             ALU.add).then_inc(s_xbo, 1)
                    for k, at in ((0, LN1), (1, LN2), (2, LN3), (3, LN4)):
                        if (late if k else t) == at + 1:
                            power(k, LN_USE[k, b] + 1)
                    if t == WKV + 5:
                        gp.wait_ge(s_wgt, 2 * b + 2)
                        gp.wait_ge(s_a_read, A_USE["ctx", b] + 1)
                        if b >= 1:
                            gp.wait_ge(s_y, b)
                        gp.tensor_tensor(new_v[:, 0], wgt[:, 1], ctx_t[b % 3][:, :, :], ALU.mult).then_inc(s_pool, 1)
                        gp.tensor_tensor(new_v[:, 1], wgt[:, 3], ctx_t[b % 3][:, :, :], ALU.mult).then_inc(s_newv, 1)
                        npool[0] += 1
                    if t == WKV + 9:
                        gp.wait_ge(s_state, b + 1)
                        own(gp.tensor_tensor(y_old[:], wgt[:, 2], num[:, :, 0:T], ALU.mult))
                        gp.tensor_tensor(y_num[:], y_old[:], new_v[:, 1], ALU.add).then_inc(s_ynum, 1)
                    if late == X2T:
                        gp.wait_ge(s_x2, b + 1)
                        if b >= 1:
                            gp.wait_ge(s_var, LN_USE[3, b - 1] + 1)
                        for i in range(TT):
                            gp.tensor_tensor(x2_beta[:, i, :], x2[b % 2][:, i, :], beta_sb[:, :],
                                             ALU.add).then_inc(s_x2b, 1)

        @block.vector
        def _(dve):
            nvec = [0]

            def own(ins):
                ins.then_inc(s_vec, 1)
                nvec[0] += 1

            def settle():
                dve.wait_ge(s_vec, nvec[0])

            def statistics(k, src):
                for i in range(TT):
                    own(nc.vector.bn_stats(stats[k][:, i, :], src[:, i, :]))

            def variance(k):
                settle()
                for i in range(TT):
                    own(nc.vector.bn_aggr(mean_var[k][:, i, :], stats[k][:, i, :]))
                settle()
                nc.vector.tensor_scalar(var_eps[k][:], mean_var[k][:, :, 1], EPS, None,
                                        ALU.add).then_inc(s_var, 1)

            def normalise(k, b, src, dst, done):
                dve.wait_ge(s_rstd, LN_USE[k, b] + 1)
                for i in range(TT):
                    last = nc.vector.tensor_scalar(dst[:, i, :], src[:, i, :], mean_var[k][:, i, 0:1],
                                                   rstd[k][:, i:i + 1], ALU.subtract, ALU.mult)
                last.then_inc(done, 1)

            dve.wait_ge(s_wqk, 32)
            for c in range(CT):
                nc.vector.tensor_copy(wq_cols[:, c, :].rearrange("p (g d h) -> p g h d", g=NSET, d=HD),
                                      wq_sb[:, c, :].rearrange("p (g h d) -> p g h d", g=NSET, d=HD)) \
                    .then_inc(s_wcols, 1)
                nc.vector.tensor_copy(wk_cols[:, c, :].rearrange("p (d h) -> p h d", d=HD),
                                      wk_sb[:, c, :].rearrange("p (h d) -> p h d", d=HD)).then_inc(s_wcols, 1)

            for tick in TICKS:
                for b in range(B):
                    for g in range(NSET):
                        i = tick - b * PERIOD - MAXIMA - g * UNITS
                        if 0 <= i < UNITS:
                            s = NSET * b + g
                            n = UNITS * s + i
                            j, qt, half = i // 4, (i // 2) % 2, i % 2
                            dve.wait_ge(s_max_mm, n + 1)
                            h = REP * j + 2 * half
                            nc.vector.tensor_reduce(neg_max[s % 2][:, qt, h:h + 2], ps_max[n % 2][:, :, :], AX,
                                                    ALU.max, negate=True).then_inc(s_max, 1)
                for b in range(B):
                    t = tick - b * PERIOD
                    late = t - LATE[b]
                    if t == QP:
                        dve.wait_ge(s_q1, NSET * (b + 1))
                        if b >= 1:
                            dve.wait_ge(s_q3, b)
                        for g in range(NSET):
                            last = nc.vector.scalar_tensor_tensor(q_rest[:, g, :], ps_a[:, g * T:g * T + T],
                                                                  bq_sb[:, g:g + 1], q_parts[:, g, 0, :],
                                                                  ALU.add, ALU.subtract)
                        last.then_inc(s_a_read, 1)
                    if t == QP + 1:
                        dve.wait_ge(s_q2, b + 1)
                        nc.vector.tensor_tensor(q_parts[:, :, 2, :], q_rest[:, :, :], q_parts[:, :, 1, :],
                                                ALU.subtract).then_inc(s_q3, 1)
                    if t == KV:
                        if b < 3:
                            dve.wait_ge(s_const, 7)
                        else:
                            dve.wait_ge(s_pv, 4 * NSET * (b - 2))
                        dve.wait_ge(s_k1, b + 1)
                        nc.vector.tensor_tensor(
                            v_cols[b % 3][:, :, :, 0:HD],
                            ps_a[:, T:T + TT * KVD].rearrange("p (i g d) -> p i g d", i=TT, d=HD),
                            bv_sb[:, :].rearrange("p (i g d) -> p i g d", i=1, d=HD).broadcast_to([P, TT, NG, HD]),
                            ALU.add).then_inc(s_v, 1)
                        nc.vector.scalar_tensor_tensor(k_rest[:, :], ps_a[0:KVD, 0:T], bk_sb[:, 0:1],
                                                       k_parts[:, 0, :], ALU.add, ALU.subtract).then_inc(s_a_read, 1)
                    if t == KV + 1:
                        dve.wait_ge(s_k2, b + 1)
                        nc.vector.tensor_tensor(k_parts[:, 2, :], k_rest[:, :], k_parts[:, 1, :],
                                                ALU.subtract).then_inc(s_k3, 1)
                    for g in range(NSET):
                        s = NSET * b + g
                        i = t - MAXIMA - g * UNITS
                        if i == UNITS - 1:
                            dve.wait_ge(s_max, UNITS * (s + 1))
                            if s >= 1:
                                dve.wait_ge(s_a, A_USE[f"m{(s - 1) % NSET}", (s - 1) // NSET] + 1)
                            own(nc.vector.tensor_copy(max_parts[:, :, 0, :], neg_max[s % 2][:, :, :]))
                            settle()
                            own(nc.vector.tensor_tensor(max_rest[:], neg_max[s % 2][:, :, :],
                                                        max_parts[:, :, 0, :], ALU.subtract))
                            settle()
                            own(nc.vector.tensor_copy(max_parts[:, :, 1, :], max_rest[:]))
                            settle()
                            nc.vector.tensor_tensor(max_parts[:, :, 2, :], max_rest[:], max_parts[:, :, 1, :],
                                                    ALU.subtract).then_inc(s_mparts, 1)
                        if t == MROWS + g * UNITS:
                            dve.wait_ge(s_a, A_USE[f"m{g}", b] + 1)
                            if s >= 1:
                                dve.wait_ge(s_mrows[(s - 1) % 3], 16 * ((s - 1) // 3 + 1))
                            nc.vector.tensor_copy(max_t[:, :], ps_a_bf[0:PARTS * HS, 0:T]).then_inc(s_a_read, 1)
                        for pair in range(2):
                            if t == heads_out(g, pair) + 3:
                                dve.wait_ge(s_headst, 2 * s + pair + 1)
                                if g == 0 and pair == 0 and b >= 1:
                                    dve.wait_ge(s_a, A_USE["att", b - 1] + 1)
                                view = ps_heads[pair][:, :].rearrange("p (r i j d) -> p r i j d", r=2, i=TT, d=32)
                                own(nc.vector.reciprocal(
                                    inv_sum[pair][:].rearrange("p r i j -> p (r i j)"),
                                    ps_heads[pair][:, :].rearrange("p (x d) -> p x d", d=32)[:, :, HD]))
                                settle()
                                for i in range(TT):
                                    dst = att[:, i, (GS * g) * REP * HD:(GS * g + GS) * REP * HD] \
                                        .rearrange("p (j r d) -> p r j d", j=GS, r=REP)[:, 2 * pair:2 * pair + 2]
                                    last = nc.vector.tensor_tensor(
                                        dst, view[:, :, i, :, 0:HD],
                                        inv_sum[pair][:, :, i, :].rearrange("p r (j d) -> p r j d", d=1)
                                        .broadcast_to([P, 2, GS, HD]), ALU.mult)
                                last.then_inc(s_att, 1)
                    if t == LN1:
                        dve.wait_ge(s_a, A_USE["op", b] + 1)
                        dve.wait_ge(s_xbo, TT * (b + 1))
                        nc.vector.tensor_tensor(flat(h1[:, :, :]), ps_a[:, :], flat(x_bo[:, :, :]),
                                                ALU.add).then_inc(s_a_read, 1)
                        dve.wait_ge(s_a_read, A_USE["op", b] + 1)
                        statistics(0, h1)
                    if t == LN1 + 3:
                        normalise(0, b, h1, x1, s_x1)
                    if t == WKV:
                        dve.wait_ge(s_a_read, A_USE["x1", b] + 1)
                        if b == 0:
                            dve.wait_ge(s_w_post, 16 * 10)
                            dve.wait_ge(s_const, 7)
                        for c in range(CT):
                            own(nc.vector.tensor_tensor_scan(top[:, c, 1:T + 1],
                                                             decay_sb[:, c:c + 1].broadcast_to([P, T]),
                                                             x1_t[:, c, :], NEG, ALU.add, ALU.max))
                    if t == WKV + 1:
                        settle()
                        if b >= 1:
                            dve.wait_ge(s_wgt, 2 * b)
                        for c in range(CT):
                            own(nc.vector.scalar_tensor_tensor(arg[:, 0, c, :], top[:, c, 0:T], decay_sb[:, c:c + 1],
                                                               top[:, c, 1:T + 1], ALU.add, ALU.subtract))
                        settle()
                        nc.vector.tensor_tensor(arg[:, 1], x1_t[:, :, :], top[:, :, 1:T + 1],
                                                ALU.subtract).then_inc(s_arg, 1)
                    if t == WKV + 2:
                        for c in range(CT):
                            own(nc.vector.scalar_tensor_tensor(gap[:, c, :], x1_t[:, c, :], bonus_sb[:, c:c + 1],
                                                               top[:, c, 0:T], ALU.add, ALU.subtract))
                        settle()
                        own(nc.vector.tensor_scalar(arg[:, 2], gap[:], 0.0, -1.0, ALU.max, ALU.mult))
                        settle()
                        nc.vector.tensor_scalar(arg[:, 3], gap[:], 0.0, None, ALU.min).then_inc(s_arg, 1)
                    if t == WKV + 6:
                        dve.wait_ge(s_wgt, 2 * b + 1)
                        for c in range(CT):
                            own(nc.vector.tensor_tensor_scan(den[:, c, 1:T + 1], wgt[:, 0, c, :], wgt[:, 1, c, :],
                                                             0.0, ALU.mult, ALU.add))
                    if t == WKV + 7:
                        dve.wait_ge(s_wgt, 2 * b + 2)
                        settle()
                        own(nc.vector.tensor_tensor(y_den[:], wgt[:, 2], den[:, :, 0:T], ALU.mult))
                        settle()
                        own(nc.vector.tensor_tensor(y_den[:], y_den[:], wgt[:, 3], ALU.add))
                    if t == WKV + 8:
                        dve.wait_ge(s_newv, b + 1)
                        settle()
                        for c in range(CT):
                            ins = nc.vector.tensor_tensor_scan(num[:, c, 1:T + 1], wgt[:, 0, c, :],
                                                               new_v[:, 0, c, :], 0.0, ALU.mult, ALU.add)
                        ins.then_inc(s_state, 1)
                    if WKV + 9 <= t < WKV + 13:
                        if t == WKV + 9:
                            settle()
                        q = slice((t - WKV - 9) * T // 2, (t - WKV - 8) * T // 2)
                        own(nc.vector.reciprocal(flat(y_inv[:, :, :])[:, q], flat(y_den[:, :, :])[:, q]))
                    if t == WKV + 13:
                        dve.wait_ge(s_ynum, b + 1)
                        settle()
                        nc.vector.tensor_tensor(y_t[:], y_num[:], y_inv[:], ALU.mult).then_inc(s_y, 1)
                    if late == LN2:
                        dve.wait_ge(s_a, A_USE["y", b] + 1)
                        nc.vector.tensor_tensor(flat(h2[:, :, :]), ps_a[:, :], flat(x1[:, :, :]),
                                                ALU.add).then_inc(s_a_read, 1)
                        dve.wait_ge(s_a_read, A_USE["y", b] + 1)
                        statistics(1, h2)
                    if late == LN2 + 3:
                        normalise(1, b, h2, x2[b % 2], s_x2)
                    if late in (EXPERT, EXPERT + 2):
                        i = (late - EXPERT) // 2
                        dve.wait_ge(s_b, B_USE[f"expert{i}", b] + 1)
                        own(nc.vector.max(top8[:, i, :], ps_b[:, D:D + NE]))
                        settle()
                        nc.vector.tensor_tensor(route[:, i:i + 1], top8[:, i, 0:1], top8[:, i, 1:2],
                                                ALU.add).then_inc(s_route, 1)
                    if late == LN3:
                        dve.wait_ge(s_b, B_USE["down", b] + 1)
                        dve.wait_ge(s_b_read, B_USE["expert1", b] + 1)
                        nc.vector.tensor_tensor(flat(h3[:, :, :]), ps_b[:, :], flat(expert_out[:, :, :]),
                                                ALU.add).then_inc(s_b_read, 1)
                        dve.wait_ge(s_b_read, B_USE["down", b] + 1)
                        statistics(2, h3)
                    for k, at in ((0, LN1), (1, LN2), (2, LN3), (3, LN4)):
                        if (late if k else t) == at + 1:
                            variance(k)
                    if late == LN3 + 1:
                        for i in range(TT):
                            own(nc.vector.scalar_tensor_tensor(h3g[:, i, :], h3[:, i, :], mean_var[2][:, i, 0:1],
                                                               gamma_sb[:, :], ALU.subtract, ALU.mult))
                    if late == LN4:
                        dve.wait_ge(s_rstd, LN_USE[2, b] + 1)
                        dve.wait_ge(s_x2b, TT * (b + 1))
                        settle()
                        for i in range(TT):
                            own(nc.vector.scalar_tensor_tensor(h4[:, i, :], h3g[:, i, :], rstd[2][:, i:i + 1],
                                                               x2_beta[:, i, :], ALU.mult, ALU.add))
                        settle()
                        statistics(3, h4)
                    if late == LN4 + 3:
                        if b >= 1:
                            dve.wait_ge(s_store, 16 * b)
                        normalise(3, b, h4, y_out, s_out)


INPUTS = ["x", "ctx_2048", "L0_attn_Wq", "L0_attn_bq", "L0_attn_Wk", "L0_attn_bk", "L0_attn_Wv", "L0_attn_bv",
          "L0_attn_Wo", "L0_attn_bo", "L0_xattn_w", "L0_xattn_u", "L0_ffn_gate_w", "L0_ffn_up_w",
          "L0_ffn_down_w", "L0_ffn_expert_weight", "L0_ffn_ln_gamma", "L0_ffn_ln_beta"]


def kernel(**inputs):
    import concourse.bacc as bacc
    from concourse.bass_utils import run_bass_kernel_spmd

    nc = bacc.Bacc("TRN2", target_bir_lowering=False, num_devices=1)
    arrays, args = {}, []
    for name in INPUTS:
        a = np.ascontiguousarray(inputs[name])
        arrays[f"in_{name}"] = a
        args.append(nc.dram_tensor(f"in_{name}", a.shape, mybir.dt.from_np(a.dtype), kind="ExternalInput").ap())
    shape = arrays["in_x"].shape
    args.append(nc.dram_tensor("out_y", shape, mybir.dt.float32, kind="ExternalOutput").ap())
    decoder_layer(nc, *args)
    r = run_bass_kernel_spmd(nc, [arrays], core_ids=[0])
    return r.results[0]["out_y"]
```

```python
import concourse.bass as bass
from concourse import mybir
from contextlib import ExitStack
import numpy as np


def decoder_layer(nc, x, ctx, wq, bq, wk, bk, wv, bv, wo, bo, w_decay, u_bonus,
                  gate_w, up_w, down_w, expert_w, ln_gamma, ln_beta, out):
    fp32, bf16 = mybir.dt.float32, mybir.dt.bfloat16
    ALU = mybir.AluOpType
    ACT = mybir.ActivationFunctionType
    AX = mybir.AxisListType.X

    B, T, D = x.shape
    P = 128
    TT = T // P
    CT = D // P
    KVD = wk.shape[1]
    HD = 8
    NG = KVD // HD
    REP = D // KVD
    GS = 4
    NSET = NG // GS
    HS = GS * REP
    PARTS = 3
    BLOCKS = [(0, 0), (0, 1), (1, 0), (0, 2), (1, 1), (2, 0)]
    QK = len(BLOCKS) * HD
    QKP = 96
    QKM = QKP + PARTS
    SCALE = float(np.float32(1.0) / np.sqrt(np.float32(HD)))
    NI = up_w.shape[1] // P
    NE = gate_w.shape[1]
    EPS = 1e-5
    NEG = -1e38
    UNITS = 16

    PERIOD = NSET * UNITS
    XT, KP, QP = -43, -35, -33
    V = -31
    ROWS = [-17, -6]
    CTXT = -23
    MAXIMA = -UNITS
    MROWS = 2
    EXP = 7
    PV_LAG = 2
    AOT, OP, LN1 = 45, 47, 48
    X1T = 54
    WKV = 55
    YT = 77
    LN2 = 78
    X2T, EXPERT, UP = 82, 84, 88
    DOWN = 98
    LN3, LN4 = 108, 114
    STORE = 125
    EARLY = [0, 0, 2, -2]
    MID = [0, 0, 0, 2]
    LATE = [-1, -1, 0, -5]
    MLP = [-1, 1, 9, -1]
    END = [-1, -1, 4, -2]
    TICKS = range(XT, (B - 1) * PERIOD + STORE + 1)

    ectx = ExitStack()
    with ectx:
        def sb(name, shape, dt=fp32):
            return ectx.enter_context(nc.sbuf_tensor(name, shape, dt))

        def ps(name, shape, dt=fp32):
            return ectx.enter_context(nc.psum_tensor(name, shape, dt))

        def sem(name):
            return ectx.enter_context(nc.semaphore(name))

        wq_sb = sb("wq_sb", [P, CT, D])
        wk_sb = sb("wk_sb", [P, CT, KVD])
        wq_cols = sb("wq_cols", [P, CT, D])
        wk_cols = sb("wk_cols", [P, CT, KVD])
        wv_sb = sb("wv_sb", [P, CT, KVD])
        wo_sb = sb("wo_sb", [P, CT, D])
        up_sb = sb("up_sb", [P, CT, NI * P])
        down_sb = sb("down_sb", [P, NI, D])
        expert_sb = sb("expert_sb", [P, CT, D + NE])
        bq_sb = sb("bq_sb", [P, NSET])
        bk_sb = sb("bk_sb", [KVD, 1])
        bv_sb = sb("bv_sb", [P, KVD])
        bo_sb = sb("bo_sb", [P, D])
        decay_sb = sb("decay_sb", [P, CT])
        bonus_sb = sb("bonus_sb", [P, CT])
        gamma_sb = sb("gamma_sb", [P, D])
        beta_sb = sb("beta_sb", [P, D])
        ident = sb("ident", [P, P])
        ident_bf = sb("ident_bf", [P, P], bf16)
        minus_half = sb("minus_half", [P, TT])

        x_in = [sb(f"x_in{b}", [P, TT, D]) for b in range(B)]
        ctx_in = [sb(f"ctx_in{b}", [P, TT, D]) for b in range(B)]
        x_t = sb("x_t", [P, CT, T])
        ctx_t = [sb(f"ctx_t{i}", [P, CT, T]) for i in range(3)]
        q_parts = sb("q_parts", [P, NSET, PARTS, T], bf16)
        q_rest = sb("q_rest", [P, NSET, T])
        k_parts = sb("k_parts", [KVD, PARTS, T], bf16)
        k_rest = sb("k_rest", [KVD, T])
        q_rows = [sb(f"q_rows{i}", [P, HS, T], bf16) for i in range(3)]
        k_rows = [sb(f"k_rows{i}", [P, NG, T], bf16) for i in range(2)]
        v_cols = [sb(f"v_cols{i}", [P, TT, NG, 32]) for i in range(3)]
        neg_max = [sb(f"neg_max{i}", [P, TT, HS]) for i in range(2)]
        max_rest = sb("max_rest", [P, TT, HS])
        max_parts = sb("max_parts", [P, TT, PARTS, HS], bf16)
        max_t = sb("max_t", [PARTS * HS, T], bf16)
        probs = [sb(f"probs{i}", [P, 2 * T]) for i in range(8)]
        heads_t = [sb(f"heads_t{i}", [P, 2 * T]) for i in range(2)]
        inv_sum = [sb(f"inv_sum{i}", [P, 2, TT, GS]) for i in range(2)]
        att = sb("att", [P, TT, D])
        att_t = sb("att_t", [P, CT, T])
        x_bo = sb("x_bo", [P, TT, D])
        h1 = sb("h1", [P, TT, D])
        x1 = sb("x1", [P, TT, D])
        x1_t = sb("x1_t", [P, CT, T])
        top = sb("top", [P, CT, T + 1])
        num = sb("num", [P, CT, T + 1])
        den = sb("den", [P, CT, T + 1])
        arg = sb("arg", [P, 4, CT, T])
        wgt = sb("wgt", [P, 4, CT, T])
        gap = sb("gap", [P, CT, T])
        new_v = sb("new_v", [P, 2, CT, T])
        y_num = sb("y_num", [P, CT, T])
        y_old = sb("y_old", [P, CT, T])
        y_den = sb("y_den", [P, CT, T])
        y_inv = sb("y_inv", [P, CT, T])
        y_t = sb("y_t", [P, CT, T])
        h2 = sb("h2", [P, TT, D])
        x2 = [sb(f"x2_{i}", [P, TT, D]) for i in range(2)]
        x2_beta = sb("x2_beta", [P, TT, D])
        x2_t = sb("x2_t", [P, CT, T])
        top8 = sb("top8", [P, TT, 8])
        route = sb("route", [P, TT])
        expert_out = sb("expert_out", [P, TT, D])
        relu_t = [sb(f"relu_t{i}", [P, 2, T]) for i in range(2)]
        inner_t = sb("inner_t", [P, NI, T])
        h3 = sb("h3", [P, TT, D])
        h3g = sb("h3g", [P, TT, D])
        h4 = sb("h4", [P, TT, D])
        y_out = sb("y_out", [P, TT, D])
        stats = [sb(f"stats{i}", [P, TT, 6]) for i in range(4)]
        mean_var = [sb(f"mean_var{i}", [P, TT, 2]) for i in range(4)]
        var_eps = [sb(f"var_eps{i}", [P, TT]) for i in range(4)]
        rstd = [sb(f"rstd{i}", [P, TT]) for i in range(4)]

        ps_max = [ps(f"ps_max{i}", [P, 2, T]) for i in range(2)]
        ps_exp = [ps(f"ps_exp{i}", [P, 2 * T]) for i in range(2)]
        ps_heads = [ps(f"ps_heads{i}", [P, 2 * T]) for i in range(2)]
        ps_a = ps("ps_a", [P, 2 * T])
        ps_b = ps("ps_b", [P, 2 * T])
        ps_a_bf = ps_a[:, 0:T].bitcast(bf16)

        s_wqk = sem("s_wqk")
        s_wv = sem("s_wv")
        s_bias = sem("s_bias")
        s_wcols = sem("s_wcols")
        s_w_post = sem("s_w_post")
        s_q0 = sem("s_q0")
        s_q0_read = sem("s_q0_read")
        s_x = [sem(f"s_x_in{b}") for b in range(B)]
        s_ctx = [sem(f"s_ctx_in{b}") for b in range(B)]
        s_ident = sem("s_ident")
        s_zero = sem("s_zero")
        s_ones = sem("s_ones")
        s_const = sem("s_const")
        s_a = sem("s_a")
        s_a_read = sem("s_a_read")
        s_ffn = [sem(f"s_ffn{i}") for i in range(6)]
        s_ffn_read = [sem(f"s_ffn_read{i}") for i in range(6)]
        s_k1, s_q1 = sem("s_k1"), sem("s_q1")
        s_k2, s_q2 = sem("s_k2"), sem("s_q2")
        s_k3, s_q3 = sem("s_k3"), sem("s_q3")
        s_rows = [sem(f"s_rows{i}") for i in range(3)]
        s_krows = [sem(f"s_krows{i}") for i in range(2)]
        s_max_mm = sem("s_max_mm")
        s_max = sem("s_max")
        s_mparts = sem("s_mparts")
        s_mrows = [sem(f"s_mrows{i}") for i in range(3)]
        s_exp_mm = sem("s_exp_mm")
        s_exp = sem("s_exp")
        s_pv = sem("s_pv")
        s_heads = sem("s_heads")
        s_headst = sem("s_headst")
        s_att = sem("s_att")
        s_xbo = sem("s_xbo")
        s_var = sem("s_var")
        s_rstd = sem("s_rstd")
        s_x1 = sem("s_x1")
        s_arg = sem("s_arg")
        s_wgt = sem("s_wgt")
        s_newv = sem("s_newv")
        s_state = sem("s_state")
        s_ynum = sem("s_ynum")
        s_den = sem("s_den")
        s_yden = sem("s_yden")
        s_y = sem("s_y")
        s_x2 = sem("s_x2")
        s_x2b = sem("s_x2b")
        s_route = sem("s_route")
        s_inner = sem("s_inner")
        s_out = sem("s_out")
        s_store = sem("s_store")
        s_vec = sem("s_vec")
        s_pool = sem("s_pool")

        def flat(ap):
            return ap.rearrange("p a b -> p (a b)")

        def row(ap):
            return ap.rearrange("(a n) -> a n", a=1)

        def shift(at, b):
            for first, shifts in ((DOWN, END), (EXPERT, MLP), (YT, LATE), (AOT, MID), (MAXIMA, [0] * B)):
                if at >= first:
                    return shifts[b]
            return EARLY[b]

        def in_order(steps, elsewhere=()):
            order = [(name, b) for tick in TICKS for b in range(B) for name, at in steps
                     if tick - b * PERIOD - shift(at, b) == at and (name, b) not in elsewhere]
            return {step: i for i, step in enumerate(order)}

        A_USE = in_order((("x", XT), ("q", QP), ("k", KP), ("v", V), ("ctx", CTXT), ("m0", MROWS),
                          ("m1", MROWS + UNITS),
                          ("att", AOT), ("op", OP), ("x1", X1T), ("y", YT), ("x2", X2T)),
                         elsewhere=[("q", 0)])
        FFN_STEPS = (("expert0", EXPERT), ("expert1", EXPERT + 2), *((f"up{i}", UP + i) for i in range(0, NI, 2)),
                     ("down0", DOWN), ("down1", DOWN + 4))
        LN_USE = in_order(((0, LN1), (1, LN2), (2, LN3), (3, LN4)))

        def heads_out(g, pair):
            return EXP + g * UNITS + 8 * pair + 8 + PV_LAG

        ffn_banks = [ps_b[:, :], flat(ps_max[0][:, :, :]), flat(ps_max[1][:, :, :]), ps_exp[0][:, :], ps_exp[1][:, :],
                     ps_heads[1][:, :]]

        def ffn_bank(name, b):
            if b < B - 2:
                return 0
            if name.startswith("up"):
                return 3 + int(name[2:]) // 2 % 2
            return {"expert0": 1, "expert1": 2, "down0": 0, "down1": 5}[name]

        FFN_USE = {}
        for k in range(len(ffn_banks)):
            uses = [step for step in in_order(FFN_STEPS) if ffn_bank(*step) == k]
            FFN_USE.update({step: i for i, step in enumerate(uses)})

        def ffn_filled(engine, name, b):
            engine.wait_ge(s_ffn[ffn_bank(name, b)], FFN_USE[name, b] + 1)

        def ffn_read(engine, name, b):
            engine.wait_ge(s_ffn_read[ffn_bank(name, b)], FFN_USE[name, b] + 1)

        def down_part(b, i):
            k = ffn_bank(f"down{i}", b)
            return ffn_banks[k][:, i * D:i * D + D] if k == 0 else ffn_banks[k][:, 0:D]

        def q_bank(b):
            if b == 0:
                return ps_heads[0], s_q0, s_q0_read, 1
            return ps_a, s_a, s_a_read, A_USE["q", b] + 1

        block = ectx.enter_context(nc.Block())

        @block.sync
        def _(sp):
            def token_tiles(a):
                return a.rearrange("(t p) c -> p t c", p=P)

            sp.dma_start(x_in[0][:], token_tiles(x[0])).then_inc(s_x[0], 16)
            sp.dma_start(wk_sb[:], token_tiles(wk)).then_inc(s_wqk, 16)
            sp.dma_start(wq_sb[:], token_tiles(wq)).then_inc(s_wqk, 16)
            sp.dma_start(bk_sb[:], bk.rearrange("(h d) -> d h", d=HD),
                         allow_slow_non_contiguous=True).then_inc(s_bias, 16)
            for g in range(NSET):
                sp.dma_start(bq_sb[:, g:g + 1], bq[g * P:g * P + P].rearrange("(h d) -> d h", d=HD),
                             allow_slow_non_contiguous=True).then_inc(s_bias, 16)
            sp.dma_start(wv_sb[:], token_tiles(wv)).then_inc(s_wv, 16)
            sp.dma_start(bv_sb[:], row(bv).broadcast_to([P, KVD])).then_inc(s_bias, 16)
            sp.dma_start(ctx_in[0][:], token_tiles(ctx[0])).then_inc(s_ctx[0], 16)

            def load_the_rest():
                for b in range(1, B):
                    sp.dma_start(x_in[b][:], token_tiles(x[b])).then_inc(s_x[b], 16)
                    sp.dma_start(ctx_in[b][:], token_tiles(ctx[b])).then_inc(s_ctx[b], 16)
                for dst, src in ((wo_sb[:], wo), (up_sb[:], up_w), (down_sb[:], down_w),
                                 (expert_sb[:, :, 0:D], expert_w), (expert_sb[:, :, D:D + NE], gate_w)):
                    sp.dma_start(dst, token_tiles(src)).then_inc(s_w_post, 16)
                for dst, src in ((bo_sb, bo), (gamma_sb, ln_gamma), (beta_sb, ln_beta)):
                    sp.dma_start(dst[:], row(src).broadcast_to([P, D])).then_inc(s_w_post, 16)
                for dst, src in ((decay_sb, w_decay), (bonus_sb, u_bonus)):
                    sp.dma_start(dst[:], src.rearrange("(c p) -> p c", p=P),
                                 allow_slow_non_contiguous=True).then_inc(s_w_post, 16)

            def rows_of_set(b, g):
                s = NSET * b + g
                if g == 0:
                    sp.wait_ge(s_ones, min(b, 1) + 1)
                    if b >= 2:
                        sp.wait_ge(s_exp_mm, UNITS * NSET * (b - 1))
                    for r, (_, kp) in sorted(enumerate(BLOCKS), key=lambda block: block[1][1]):
                        sp.wait_ge((s_k1, s_k2, s_k3)[kp], b + 1)
                        sp.dma_start(k_rows[b % 2][HD * r:HD * r + HD, :, :],
                                     k_parts[:, kp, :]).then_inc(s_krows[b % 2], 16)
                sp.wait_ge(s_zero, min(s, 2) + 1)
                if s >= 3:
                    sp.wait_ge(s_exp_mm, UNITS * (s - 2))
                for r, (qp, _) in sorted(enumerate(BLOCKS), key=lambda block: block[1][0]):
                    if qp == 0:
                        sp.wait_ge(s_q1, NSET * b + g + 1)
                    else:
                        sp.wait_ge((s_q2, s_q3)[qp - 1], b + 1)
                    sp.dma_start(q_rows[s % 3][HD * r:HD * r + HD, :, :],
                                 q_parts[:, g, qp, :]).then_inc(s_rows[s % 3], 16)

            for tick in TICKS:
                for b in range(B):
                    t = tick - b * PERIOD
                    early, mid, late, mlp, end = t - EARLY[b], t - MID[b], t - LATE[b], t - MLP[b], t - END[b]
                    for g in range(NSET):
                        if early == ROWS[g]:
                            rows_of_set(b, g)
                            if b == 0 and g == 0:
                                load_the_rest()
                        if t == MROWS + g * UNITS + 1:
                            s = NSET * b + g
                            sp.wait_ge(s_a_read, A_USE[f"m{g}", b] + 1)
                            sp.dma_start(q_rows[s % 3][QKP:QKM, :, :],
                                         max_t[:, :]).then_inc(s_mrows[s % 3], 16)
                    if end == STORE:
                        if b < B - 1:
                            sp.wait_ge(s_out, b + 1)
                            sp.dma_start(token_tiles(out[b]), y_out[:]).then_inc(s_store, 16)
                        else:
                            for i in range(TT):
                                sp.wait_ge(s_out, b + i + 1)
                                sp.dma_start(out[b, i * P:i * P + P, :], y_out[:, i, :]).then_inc(s_store, 16)
            sp.wait_ge(s_store, 16 * (B - 1 + TT))

        @block.tensor
        def _(pe):
            def open_a(use):
                if A_USE[use] >= 1:
                    pe.wait_ge(s_a_read, A_USE[use])

            def open_ffn(name, b):
                k, n = ffn_bank(name, b), FFN_USE[name, b]
                if n >= 1:
                    pe.wait_ge(s_ffn_read[k], n)
                elif k in (1, 2):
                    pe.wait_ge(s_max, UNITS * NSET * B)
                elif k in (3, 4):
                    pe.wait_ge(s_exp, UNITS * NSET * B)
                elif k == 5:
                    pe.wait_ge(s_att, 2 * NSET * B)

            def transposes(src):
                for c in range(CT):
                    for i in range(TT):
                        last = nc.tensor.transpose(ps_a[:, c * T + i * P:c * T + i * P + P],
                                                   src[:, i, c * P:c * P + P], ident[:, :])
                last.then_inc(s_a, 1)

            def maxima_unit(b, g, i):
                s, n = NSET * b + g, UNITS * (NSET * b + g) + i
                j, qt, half = i // 4, (i // 2) % 2, i % 2
                if i == 0:
                    pe.wait_ge(s_rows[s % 3], 16 * len(BLOCKS) * (s // 3 + 1))
                    if g == 0:
                        pe.wait_ge(s_krows[b % 2], 16 * len(BLOCKS) * (b // 2 + 1))
                if n >= 2:
                    pe.wait_ge(s_max, n - 1)
                for r in range(2):
                    last = nc.tensor.matmul(ps_max[n % 2][:, r, :],
                                            q_rows[s % 3][0:QKP, REP * j + 2 * half + r, qt * P:qt * P + P],
                                            k_rows[b % 2][0:QKP, GS * g + j, :], start=True, stop=True)
                last.then_inc(s_max_mm, 1)

            def exp_unit(b, g, i):
                s, n = NSET * b + g, UNITS * (NSET * b + g) + i
                pair, kt, j = i // 8, (i // 4) % 2, i % 4
                if i == 0:
                    pe.wait_ge(s_mrows[s % 3], 16 * (s // 3 + 1))
                if n >= 2:
                    pe.wait_ge(s_exp, n - 1)
                nc.tensor.matmul(ps_exp[n % 2][:, :], k_rows[b % 2][0:QKM, GS * g + j, kt * P:kt * P + P],
                                 q_rows[s % 3][0:QKM, REP * j + 2 * pair:REP * j + 2 * pair + 2, :]
                                 .rearrange("p h t -> p (h t)"), start=True, stop=True).then_inc(s_exp_mm, 1)

            def pv_group(b, g, i):
                s, n = NSET * b + g, 4 * (NSET * b + g) + i
                pair, kt = i // 2, i % 2
                if i == 0 and g == 0:
                    pe.wait_ge(s_a_read, A_USE["v", b] + 1)
                pe.wait_ge(s_exp, 4 * n + 4)
                if s == 0 and i == 0:
                    pe.wait_ge(s_q0_read, 1)
                if kt == 0 and s >= 1:
                    pe.wait_ge(s_att, 2 * (s - 1) + pair + 1)
                for j in range(GS):
                    last = nc.tensor.matmul(ps_heads[pair][32 * j:32 * j + 32, :],
                                            v_cols[b % 3][:, kt, GS * g + j, :], probs[(4 * n + j) % 8][:, :],
                                            start=(kt == 0), stop=(kt == 1))
                last.then_inc(s_pv, 1)

            pe.wait_ge(s_ident, 2)
            for tick in TICKS:
                for b in range(B):
                    for g in range(NSET):
                        i = tick - b * PERIOD - EXP - g * UNITS
                        if 0 <= i < UNITS:
                            exp_unit(b, g, i)
                for b in range(B):
                    for g in range(NSET):
                        i = tick - b * PERIOD - MAXIMA - g * UNITS
                        if 0 <= i < UNITS:
                            maxima_unit(b, g, i)
                for b in range(B):
                    t = tick - b * PERIOD
                    early, mid, late, mlp, end = t - EARLY[b], t - MID[b], t - LATE[b], t - MLP[b], t - END[b]
                    if early == XT:
                        pe.wait_ge(s_x[b], 16)
                        open_a(("x", b))
                        transposes(x_in[b])
                    if early == KP:
                        if b == 0:
                            pe.wait_ge(s_wcols, 2 * CT)
                        open_a(("k", b))
                        pe.wait_ge(s_a_read, A_USE["x", b] + 1)
                        for c in range(CT):
                            last = nc.tensor.matmul(ps_a[0:KVD, 0:T], wk_cols[:, c, :], x_t[:, c, :],
                                                    start=(c == 0), stop=(c == CT - 1))
                        last.then_inc(s_a, 1)
                    if early == QP:
                        bank, filled, _, _ = q_bank(b)
                        if b >= 1:
                            open_a(("q", b))
                        for g in range(NSET):
                            for c in range(CT):
                                last = nc.tensor.matmul(bank[:, g * T:g * T + T], wq_cols[:, c, g * P:g * P + P],
                                                        x_t[:, c, :], start=(c == 0), stop=(c == CT - 1))
                        last.then_inc(filled, 1)
                    if early == V:
                        if b == 0:
                            pe.wait_ge(s_wv, 16)
                        open_a(("v", b))
                        for i in range(TT):
                            for c in range(CT):
                                last = nc.tensor.matmul(ps_a[:, i * KVD:i * KVD + KVD],
                                                        x_t[:, c, i * P:i * P + P], wv_sb[:, c, :],
                                                        start=(c == 0), stop=(c == CT - 1))
                        last.then_inc(s_a, 1)
                    if early == CTXT:
                        pe.wait_ge(s_ctx[b], 16)
                        open_a(("ctx", b))
                        transposes(ctx_in[b])
                    for g in range(NSET):
                        if t == MROWS + g * UNITS:
                            s = NSET * b + g
                            open_a((f"m{g}", b))
                            pe.wait_ge(s_mparts, s + 1)
                            for i in range(TT):
                                last = nc.tensor.transpose(ps_a_bf[0:PARTS * HS, i * P:i * P + P],
                                                           max_parts[:, i, :, :].rearrange("p a b -> p (a b)"),
                                                           ident_bf[:, :])
                            last.then_inc(s_a, 1)
                    for g in range(NSET):
                        i = t - EXP - g * UNITS - 3 - PV_LAG
                        if i in (0, 4, 8, 12):
                            pv_group(b, g, i // 4)
                        for pair in range(2):
                            if t == heads_out(g, pair) + 2:
                                pe.wait_ge(s_heads, 2 * (NSET * b + g) + pair + 1)
                                for i in range(4):
                                    last = nc.tensor.transpose(ps_heads[pair][:, i * P:i * P + P],
                                                               heads_t[pair][:, i * P:i * P + P], ident[:, :])
                                last.then_inc(s_headst, 1)
                    if mid == AOT:
                        open_a(("att", b))
                        pe.wait_ge(s_att, 2 * NSET * (b + 1))
                        transposes(att)
                    if mid == OP:
                        if b == 0:
                            pe.wait_ge(s_w_post, 16 * 10)
                        open_a(("op", b))
                        pe.wait_ge(s_a_read, A_USE["att", b] + 1)
                        for i in range(TT):
                            for c in range(CT):
                                last = nc.tensor.matmul(ps_a[:, i * D:i * D + D], att_t[:, c, i * P:i * P + P],
                                                        wo_sb[:, c, :], start=(c == 0), stop=(c == CT - 1))
                        last.then_inc(s_a, 1)
                    if mid == X1T:
                        open_a(("x1", b))
                        pe.wait_ge(s_x1, b + 1)
                        transposes(x1)
                    if late == YT:
                        open_a(("y", b))
                        pe.wait_ge(s_y, b + 1)
                        transposes(y_t)
                    if late == X2T:
                        open_a(("x2", b))
                        pe.wait_ge(s_x2, b + 1)
                        transposes(x2[b % 2])
                    if mlp in (EXPERT, EXPERT + 2):
                        i = (mlp - EXPERT) // 2
                        open_ffn(f"expert{i}", b)
                        k = ffn_bank(f"expert{i}", b)
                        pe.wait_ge(s_a_read, A_USE["x2", b] + 1)
                        for c in range(CT):
                            last = nc.tensor.matmul(ffn_banks[k][:, 0:D + NE], x2_t[:, c, i * P:i * P + P],
                                                    expert_sb[:, c, :], start=(c == 0), stop=(c == CT - 1))
                        last.then_inc(s_ffn[k], 1)
                    if UP <= mlp < UP + NI:
                        m, i = mlp - UP, (mlp - UP) % 2
                        k = ffn_bank(f"up{m - i}", b)
                        if i == 0:
                            open_ffn(f"up{m}", b)
                        for c in range(CT):
                            last = nc.tensor.matmul(ffn_banks[k][:, i * T:i * T + T], up_sb[:, c, m * P:m * P + P],
                                                    x2_t[:, c, :], start=(c == 0), stop=(c == CT - 1))
                        if i == 1:
                            last.then_inc(s_ffn[k], 1)
                    if DOWN <= end < DOWN + 8:
                        i, part = (end - DOWN) // 4, (end - DOWN) % 4
                        if b == B - 1:
                            i, part = (end - DOWN) // 2 % 2, (end - DOWN) // 4 * 2 + (end - DOWN) % 2
                        if part == 0 and (i == 0 or ffn_bank("down1", b) != ffn_bank("down0", b)):
                            open_ffn(f"down{i}", b)
                        for m in range(part * NI // 4, (part + 1) * NI // 4):
                            if i == 0 and m % 2 == 0:
                                pe.wait_ge(s_inner, NI // 2 * b + m // 2 + 1)
                            last = nc.tensor.matmul(down_part(b, i), inner_t[:, m, i * P:i * P + P],
                                                    down_sb[:, m, :], start=(m == 0), stop=(m == NI - 1))
                        if part == 3:
                            last.then_inc(s_ffn[ffn_bank(f"down{i}", b)], 1)

        @block.scalar
        def _(act):
            def evacuate(name, b, dst):
                act.wait_ge(s_a, A_USE[name, b] + 1)
                nc.scalar.activation(dst, ps_a[:, :], ACT.Copy).then_inc(s_a_read, 1)

            for tick in TICKS:
                for b in range(B):
                    for g in range(NSET):
                        i = tick - b * PERIOD - EXP - g * UNITS
                        if 0 <= i < UNITS:
                            n = UNITS * (NSET * b + g) + i
                            act.wait_ge(s_exp_mm, n + 1)
                            if n >= 8:
                                act.wait_ge(s_pv, (n - 8) // 4 + 1)
                            nc.scalar.activation(probs[n % 8][:, :], ps_exp[n % 2][:, :], ACT.Exp,
                                                 scale=SCALE).then_inc(s_exp, 1)
                for b in range(B):
                    t = tick - b * PERIOD
                    early, mid, late, mlp, end = t - EARLY[b], t - MID[b], t - LATE[b], t - MLP[b], t - END[b]
                    if early == XT:
                        evacuate("x", b, flat(x_t[:, :, :]))
                    if early == KP:
                        act.wait_ge(s_a, A_USE["k", b] + 1)
                        if b == 0:
                            act.wait_ge(s_bias, 16 * (NSET + 2))
                        if b >= 1:
                            act.wait_ge(s_krows[(b - 1) % 2], 16 * len(BLOCKS) * ((b - 1) // 2 + 1))
                        nc.scalar.activation(k_parts[:, 0, :], ps_a[0:KVD, 0:T], ACT.Identity,
                                             bias=bk_sb[:, 0:1]).then_inc(s_k1, 1)
                    if early == KP + 1:
                        act.wait_ge(s_a_read, A_USE["k", b] + 1)
                        nc.scalar.activation(k_parts[:, 1, :], k_rest[:, :], ACT.Copy).then_inc(s_k2, 1)
                    if early == QP:
                        bank, filled, _, n = q_bank(b)
                        act.wait_ge(filled, n)
                        if b >= 1:
                            for s in (NSET * b - 1, NSET * b - 2):
                                act.wait_ge(s_rows[s % 3], 16 * len(BLOCKS) * (s // 3 + 1))
                        for g in range(NSET):
                            nc.scalar.activation(q_parts[:, g, 0, :], bank[:, g * T:g * T + T], ACT.Identity,
                                                 bias=bq_sb[:, g:g + 1]).then_inc(s_q1, 1)
                    if early == QP + 1:
                        _, _, read, n = q_bank(b)
                        act.wait_ge(read, n)
                        nc.scalar.activation(q_parts[:, :, 1, :], q_rest[:, :, :], ACT.Copy).then_inc(s_q2, 1)
                    if early == CTXT:
                        if b >= 3:
                            act.wait_ge(s_newv, 2 * (b - 2))
                        evacuate("ctx", b, flat(ctx_t[b % 3][:, :, :]))
                    for g in range(NSET):
                        for pair in range(2):
                            if t == heads_out(g, pair):
                                n = 2 * (NSET * b + g) + pair
                                act.wait_ge(s_pv, 2 * n + 2)
                                if n >= 2:
                                    act.wait_ge(s_headst, n - 1)
                                nc.scalar.activation(heads_t[pair][:, :], ps_heads[pair][:, :],
                                                     ACT.Copy).then_inc(s_heads, 1)
                    if mid == AOT:
                        evacuate("att", b, flat(att_t[:, :, :]))
                    if mid == X1T:
                        if b >= 1:
                            act.wait_ge(s_arg, 2 * b)
                        evacuate("x1", b, flat(x1_t[:, :, :]))
                    if mid in (WKV + 3, WKV + 4):
                        half = mid - WKV - 3
                        act.wait_ge(s_arg, 2 * b + half + 1)
                        if b >= 1:
                            act.wait_ge(s_y, b)
                        nc.scalar.activation(wgt[:, 2 * half:2 * half + 2].rearrange("p a c t -> p (a c t)"),
                                             arg[:, 2 * half:2 * half + 2].rearrange("p a c t -> p (a c t)"),
                                             ACT.Exp).then_inc(s_wgt, 1)
                    if late == X2T:
                        evacuate("x2", b, flat(x2_t[:, :, :]))
                    if mlp in (EXPERT, EXPERT + 2):
                        i = (mlp - EXPERT) // 2
                        act.wait_ge(s_route, TT * b + i + 1)
                        if i == 0 and b >= 1:
                            for n in range(TT):
                                ffn_read(act, f"down{n}", b - 1)
                        k = ffn_bank(f"expert{i}", b)
                        nc.scalar.activation(expert_out[:, i, :], ffn_banks[k][:, 0:D], ACT.Copy,
                                             scale=route[:, i:i + 1]).then_inc(s_ffn_read[k], 1)
                    if UP < mlp < UP + NI and (mlp - UP) % 2 == 1:
                        m = (mlp - UP) // 2
                        n = NI // 2 * b + m
                        ffn_filled(act, f"up{2 * m}", b)
                        if n >= 2:
                            act.wait_ge(s_inner, n - 1)
                        k = ffn_bank(f"up{2 * m}", b)
                        nc.scalar.activation(flat(relu_t[n % 2][:, :, :]), ffn_banks[k],
                                             ACT.Relu).then_inc(s_ffn_read[k], 1)
                    if UP < mlp <= UP + NI and (mlp - UP) % 2 == 0:
                        m = (mlp - UP) // 2 - 1
                        n = NI // 2 * b + m
                        ffn_read(act, f"up{2 * m}", b)
                        if m == 0 and b >= 1:
                            for i in range(TT):
                                ffn_filled(act, f"down{i}", b - 1)
                        nc.scalar.activation(flat(inner_t[:, 2 * m:2 * m + 2, :]), flat(relu_t[n % 2][:, :, :]),
                                             ACT.Square).then_inc(s_inner, 1)

        @block.gpsimd
        def _(gp):
            npool = [0]

            def own(ins):
                ins.then_inc(s_pool, 1)
                npool[0] += 1
                gp.wait_ge(s_pool, npool[0])

            own(gp.memset(ident[:], 0.0))
            gp.affine_select(out=ident[:], in_=ident[:], compare_op=ALU.not_equal, fill=1.0, base=0,
                             pattern=[[-1, P]], channel_multiplier=1).then_inc(s_ident, 1)
            gp.wait_ge(s_ident, 1)
            gp.tensor_copy(ident_bf[:], ident[:]).then_inc(s_ident, 1)
            for i in range(3):
                own(gp.memset(v_cols[i][:], 0.0))
                gp.memset(v_cols[i][:, :, :, HD:HD + 1], 1.0).then_inc(s_const, 1)
            gp.memset(minus_half[:], -0.5).then_inc(s_const, 1)
            gp.memset(top[:, :, 0:1], NEG).then_inc(s_const, 1)
            gp.memset(num[:, :, 0:1], 0.0).then_inc(s_const, 1)
            gp.memset(den[:, :, 0:1], 0.0).then_inc(s_const, 1)
            for i in range(3):
                if i < 2:
                    gp.memset(k_rows[i][:], 1.0).then_inc(s_ones, 1)
                gp.memset(q_rows[i][:].rearrange("p h t -> p (h t)").bitcast(fp32), 0.0).then_inc(s_zero, 1)
            gp.wait_ge(s_const, 7)

            def power(k, n):
                gp.wait_ge(s_var, n)
                gp.tensor_tensor(rstd[k][:], var_eps[k][:], minus_half[:], ALU.pow).then_inc(s_rstd, 1)

            for tick in TICKS:
                for b in range(B):
                    t = tick - b * PERIOD
                    early, mid, late, mlp, end = t - EARLY[b], t - MID[b], t - LATE[b], t - MLP[b], t - END[b]
                    if mid == AOT - 6:
                        if b == 0:
                            gp.wait_ge(s_w_post, 16 * 10)
                        gp.wait_ge(s_x[b], 16)
                        if b >= 1:
                            gp.wait_ge(s_var, LN_USE[0, b - 1] + 1)
                        for i in range(TT):
                            gp.tensor_tensor(x_bo[:, i, :], x_in[b][:, i, :], bo_sb[:, :],
                                             ALU.add).then_inc(s_xbo, 1)
                    for k, at in ((0, LN1), (1, LN2), (2, LN3), (3, LN4)):
                        if (mid, late, end, end)[k] == at + 1:
                            if b < B - 1 or k < 2:
                                power(k, LN_USE[k, b] + 1)
                            elif k == 3:
                                power(k, LN_USE[2, b] + TT + 1)
                            else:
                                for i in range(TT):
                                    gp.wait_ge(s_var, LN_USE[2, b] + i + 1)
                                    gp.tensor_tensor(rstd[k][:, i:i + 1], var_eps[k][:, i:i + 1],
                                                     minus_half[:, i:i + 1], ALU.pow).then_inc(s_rstd, 1)
                    if mid == WKV + 5:
                        gp.wait_ge(s_a_read, A_USE["ctx", b] + 1)
                        if b >= 1:
                            gp.wait_ge(s_y, b)
                        if b < B - 1:
                            gp.wait_ge(s_wgt, 2 * b + 1)
                            gp.tensor_tensor(new_v[:, 0], wgt[:, 1], ctx_t[b % 3][:, :, :],
                                             ALU.mult).then_inc(s_newv, 1)
                        gp.wait_ge(s_wgt, 2 * b + 2)
                        gp.tensor_tensor(new_v[:, 1], wgt[:, 3], ctx_t[b % 3][:, :, :], ALU.mult).then_inc(s_newv, 1)
                    if mid == WKV + 7 and b < B - 1:
                        gp.wait_ge(s_den, b + 1)
                        own(gp.tensor_tensor(y_den[:], wgt[:, 2], den[:, :, 0:T], ALU.mult))
                        gp.tensor_tensor(y_den[:], y_den[:], wgt[:, 3], ALU.add).then_inc(s_yden, 1)
                    if mid == WKV + 9:
                        gp.wait_ge(s_state, b + 1)
                        own(gp.tensor_tensor(y_old[:], wgt[:, 2], num[:, :, 0:T], ALU.mult))
                        gp.tensor_tensor(y_num[:], y_old[:], new_v[:, 1], ALU.add).then_inc(s_ynum, 1)
                    if end == DOWN:
                        gp.wait_ge(s_x2, b + 1)
                        if b >= 1:
                            gp.wait_ge(s_var, LN_USE[3, b - 1] + 1)
                        for i in range(TT):
                            gp.tensor_tensor(x2_beta[:, i, :], x2[b % 2][:, i, :], beta_sb[:, :],
                                             ALU.add).then_inc(s_x2b, 1)

        @block.vector
        def _(dve):
            nvec = [0]

            def own(ins):
                ins.then_inc(s_vec, 1)
                nvec[0] += 1

            def settle():
                dve.wait_ge(s_vec, nvec[0])

            def statistics(k, src):
                for i in range(TT):
                    own(nc.vector.bn_stats(stats[k][:, i, :], src[:, i, :]))

            def variance(k):
                settle()
                for i in range(TT):
                    own(nc.vector.bn_aggr(mean_var[k][:, i, :], stats[k][:, i, :]))
                settle()
                nc.vector.tensor_scalar(var_eps[k][:], mean_var[k][:, :, 1], EPS, None,
                                        ALU.add).then_inc(s_var, 1)

            def normalise(k, b, src, dst, done):
                dve.wait_ge(s_rstd, LN_USE[k, b] + 1)
                for i in range(TT):
                    last = nc.vector.tensor_scalar(dst[:, i, :], src[:, i, :], mean_var[k][:, i, 0:1],
                                                   rstd[k][:, i:i + 1], ALU.subtract, ALU.mult)
                last.then_inc(done, 1)

            def tile_variance(k, src, i):
                own(nc.vector.bn_stats(stats[k][:, i, :], src[:, i, :]))
                settle()
                own(nc.vector.bn_aggr(mean_var[k][:, i, :], stats[k][:, i, :]))
                settle()
                nc.vector.tensor_scalar(var_eps[k][:, i:i + 1], mean_var[k][:, i, 1:2], EPS, None,
                                        ALU.add).then_inc(s_var, 1)

            def numerator_scan():
                settle()
                for c in range(CT):
                    last = nc.vector.tensor_tensor_scan(num[:, c, 1:T + 1], wgt[:, 0, c, :], new_v[:, 0, c, :],
                                                        0.0, ALU.mult, ALU.add)
                last.then_inc(s_state, 1)

            dve.wait_ge(s_wqk, 32)
            for c in range(CT):
                nc.vector.tensor_copy(wq_cols[:, c, :].rearrange("p (g d h) -> p g h d", g=NSET, d=HD),
                                      wq_sb[:, c, :].rearrange("p (g h d) -> p g h d", g=NSET, d=HD)) \
                    .then_inc(s_wcols, 1)
                nc.vector.tensor_copy(wk_cols[:, c, :].rearrange("p (d h) -> p h d", d=HD),
                                      wk_sb[:, c, :].rearrange("p (h d) -> p h d", d=HD)).then_inc(s_wcols, 1)

            for tick in TICKS:
                for b in range(B):
                    for g in range(NSET):
                        i = tick - b * PERIOD - MAXIMA - g * UNITS
                        if 0 <= i < UNITS:
                            s = NSET * b + g
                            n = UNITS * s + i
                            j, qt, half = i // 4, (i // 2) % 2, i % 2
                            dve.wait_ge(s_max_mm, n + 1)
                            h = REP * j + 2 * half
                            nc.vector.tensor_reduce(neg_max[s % 2][:, qt, h:h + 2], ps_max[n % 2][:, :, :], AX,
                                                    ALU.max, negate=True).then_inc(s_max, 1)
                for b in range(B):
                    t = tick - b * PERIOD
                    early, mid, late, mlp, end = t - EARLY[b], t - MID[b], t - LATE[b], t - MLP[b], t - END[b]
                    if early == QP:
                        dve.wait_ge(s_q1, NSET * (b + 1))
                        if b >= 1:
                            dve.wait_ge(s_q3, b)
                        bank, _, read, _ = q_bank(b)
                        for g in range(NSET):
                            last = nc.vector.scalar_tensor_tensor(q_rest[:, g, :], bank[:, g * T:g * T + T],
                                                                  bq_sb[:, g:g + 1], q_parts[:, g, 0, :],
                                                                  ALU.add, ALU.subtract)
                        last.then_inc(read, 1)
                    if early == QP + 1:
                        dve.wait_ge(s_q2, b + 1)
                        nc.vector.tensor_tensor(q_parts[:, :, 2, :], q_rest[:, :, :], q_parts[:, :, 1, :],
                                                ALU.subtract).then_inc(s_q3, 1)
                    if early == V:
                        if b < 3:
                            dve.wait_ge(s_const, 7)
                        else:
                            dve.wait_ge(s_pv, 4 * NSET * (b - 2))
                        if b == 0:
                            dve.wait_ge(s_bias, 16 * (NSET + 2))
                        dve.wait_ge(s_a, A_USE["v", b] + 1)
                        nc.vector.tensor_tensor(
                            v_cols[b % 3][:, :, :, 0:HD],
                            ps_a[:, 0:TT * KVD].rearrange("p (i g d) -> p i g d", i=TT, d=HD),
                            bv_sb[:, :].rearrange("p (i g d) -> p i g d", i=1, d=HD).broadcast_to([P, TT, NG, HD]),
                            ALU.add).then_inc(s_a_read, 1)
                    if early == KP:
                        dve.wait_ge(s_k1, b + 1)
                        nc.vector.scalar_tensor_tensor(k_rest[:, :], ps_a[0:KVD, 0:T], bk_sb[:, 0:1],
                                                       k_parts[:, 0, :], ALU.add, ALU.subtract).then_inc(s_a_read, 1)
                    if early == KP + 1:
                        dve.wait_ge(s_k2, b + 1)
                        nc.vector.tensor_tensor(k_parts[:, 2, :], k_rest[:, :], k_parts[:, 1, :],
                                                ALU.subtract).then_inc(s_k3, 1)
                    for g in range(NSET):
                        s = NSET * b + g
                        i = t - MAXIMA - g * UNITS
                        if i == UNITS - 1:
                            dve.wait_ge(s_max, UNITS * (s + 1))
                            if s >= 1:
                                dve.wait_ge(s_a, A_USE[f"m{(s - 1) % NSET}", (s - 1) // NSET] + 1)
                            own(nc.vector.tensor_copy(max_parts[:, :, 0, :], neg_max[s % 2][:, :, :]))
                            settle()
                            own(nc.vector.tensor_tensor(max_rest[:], neg_max[s % 2][:, :, :],
                                                        max_parts[:, :, 0, :], ALU.subtract))
                            settle()
                            own(nc.vector.tensor_copy(max_parts[:, :, 1, :], max_rest[:]))
                            settle()
                            nc.vector.tensor_tensor(max_parts[:, :, 2, :], max_rest[:], max_parts[:, :, 1, :],
                                                    ALU.subtract).then_inc(s_mparts, 1)
                        if t == MROWS + g * UNITS:
                            dve.wait_ge(s_a, A_USE[f"m{g}", b] + 1)
                            if s >= 1:
                                dve.wait_ge(s_mrows[(s - 1) % 3], 16 * ((s - 1) // 3 + 1))
                            nc.vector.tensor_copy(max_t[:, :], ps_a_bf[0:PARTS * HS, 0:T]).then_inc(s_a_read, 1)
                        for pair in range(2):
                            if t == heads_out(g, pair) + 3:
                                dve.wait_ge(s_headst, 2 * s + pair + 1)
                                if g == 0 and pair == 0 and b >= 1:
                                    dve.wait_ge(s_a, A_USE["att", b - 1] + 1)
                                view = ps_heads[pair][:, :].rearrange("p (r i j d) -> p r i j d", r=2, i=TT, d=32)
                                own(nc.vector.reciprocal(
                                    inv_sum[pair][:].rearrange("p r i j -> p (r i j)"),
                                    ps_heads[pair][:, :].rearrange("p (x d) -> p x d", d=32)[:, :, HD]))
                                settle()
                                for i in range(TT):
                                    dst = att[:, i, (GS * g) * REP * HD:(GS * g + GS) * REP * HD] \
                                        .rearrange("p (j r d) -> p r j d", j=GS, r=REP)[:, 2 * pair:2 * pair + 2]
                                    last = nc.vector.tensor_tensor(
                                        dst, view[:, :, i, :, 0:HD],
                                        inv_sum[pair][:, :, i, :].rearrange("p r (j d) -> p r j d", d=1)
                                        .broadcast_to([P, 2, GS, HD]), ALU.mult)
                                last.then_inc(s_att, 1)
                    if mid == LN1:
                        dve.wait_ge(s_a, A_USE["op", b] + 1)
                        dve.wait_ge(s_xbo, TT * (b + 1))
                        nc.vector.tensor_tensor(flat(h1[:, :, :]), ps_a[:, :], flat(x_bo[:, :, :]),
                                                ALU.add).then_inc(s_a_read, 1)
                        dve.wait_ge(s_a_read, A_USE["op", b] + 1)
                        statistics(0, h1)
                    if mid == LN1 + 3:
                        normalise(0, b, h1, x1, s_x1)
                    if mid == WKV:
                        dve.wait_ge(s_a_read, A_USE["x1", b] + 1)
                        if b == 0:
                            dve.wait_ge(s_w_post, 16 * 10)
                            dve.wait_ge(s_const, 7)
                        for c in range(CT):
                            own(nc.vector.tensor_tensor_scan(top[:, c, 1:T + 1],
                                                             decay_sb[:, c:c + 1].broadcast_to([P, T]),
                                                             x1_t[:, c, :], NEG, ALU.add, ALU.max))
                    if mid == WKV + 1:
                        settle()
                        if b >= 1:
                            dve.wait_ge(s_wgt, 2 * b)
                        for c in range(CT):
                            own(nc.vector.scalar_tensor_tensor(arg[:, 0, c, :], top[:, c, 0:T], decay_sb[:, c:c + 1],
                                                               top[:, c, 1:T + 1], ALU.add, ALU.subtract))
                        settle()
                        nc.vector.tensor_tensor(arg[:, 1], x1_t[:, :, :], top[:, :, 1:T + 1],
                                                ALU.subtract).then_inc(s_arg, 1)
                    if mid == WKV + 2:
                        for c in range(CT):
                            own(nc.vector.scalar_tensor_tensor(gap[:, c, :], x1_t[:, c, :], bonus_sb[:, c:c + 1],
                                                               top[:, c, 0:T], ALU.add, ALU.subtract))
                        settle()
                        own(nc.vector.tensor_scalar(arg[:, 2], gap[:], 0.0, -1.0, ALU.max, ALU.mult))
                        settle()
                        nc.vector.tensor_scalar(arg[:, 3], gap[:], 0.0, None, ALU.min).then_inc(s_arg, 1)
                    if mid == WKV + 6:
                        dve.wait_ge(s_wgt, 2 * b + 1)
                        for c in range(CT):
                            last = nc.vector.tensor_tensor_scan(den[:, c, 1:T + 1], wgt[:, 0, c, :], wgt[:, 1, c, :],
                                                                0.0, ALU.mult, ALU.add)
                        last.then_inc(s_den, 1)
                        if b == B - 1:
                            dve.wait_ge(s_a_read, A_USE["ctx", b] + 1)
                            own(nc.vector.tensor_tensor(new_v[:, 0], wgt[:, 1], ctx_t[b % 3][:, :, :], ALU.mult))
                            numerator_scan()
                    if mid == WKV + 7 and b == B - 1:
                        dve.wait_ge(s_wgt, 2 * b + 2)
                        dve.wait_ge(s_den, b + 1)
                        own(nc.vector.tensor_tensor(y_den[:], wgt[:, 2], den[:, :, 0:T], ALU.mult))
                        settle()
                        own(nc.vector.tensor_tensor(y_den[:], y_den[:], wgt[:, 3], ALU.add))
                    if mid == WKV + 8 and b < B - 1:
                        dve.wait_ge(s_newv, 2 * b + 1)
                        numerator_scan()
                    if WKV + 9 <= mid < WKV + 13:
                        if mid == WKV + 9 and b < B - 1:
                            dve.wait_ge(s_yden, b + 1)
                        elif mid == WKV + 9:
                            settle()
                        q = slice((mid - WKV - 9) * T // 2, (mid - WKV - 8) * T // 2)
                        own(nc.vector.reciprocal(flat(y_inv[:, :, :])[:, q], flat(y_den[:, :, :])[:, q]))
                    if mid == WKV + 13:
                        dve.wait_ge(s_ynum, b + 1)
                        settle()
                        nc.vector.tensor_tensor(y_t[:], y_num[:], y_inv[:], ALU.mult).then_inc(s_y, 1)
                    if late == LN2:
                        dve.wait_ge(s_a, A_USE["y", b] + 1)
                        nc.vector.tensor_tensor(flat(h2[:, :, :]), ps_a[:, :], flat(x1[:, :, :]),
                                                ALU.add).then_inc(s_a_read, 1)
                        dve.wait_ge(s_a_read, A_USE["y", b] + 1)
                        statistics(1, h2)
                    if late == LN2 + 3:
                        normalise(1, b, h2, x2[b % 2], s_x2)
                    if mlp in (EXPERT, EXPERT + 2):
                        i = (mlp - EXPERT) // 2
                        ffn_filled(dve, f"expert{i}", b)
                        own(nc.vector.max(top8[:, i, :], ffn_banks[ffn_bank(f"expert{i}", b)][:, D:D + NE]))
                        settle()
                        nc.vector.tensor_tensor(route[:, i:i + 1], top8[:, i, 0:1], top8[:, i, 1:2],
                                                ALU.add).then_inc(s_route, 1)
                    if end == LN3:
                        for i in range(TT):
                            if b < B - 1:
                                ffn_filled(dve, "down1", b)
                            else:
                                ffn_filled(dve, f"down{i}", b)
                            ffn_read(dve, f"expert{i}", b)
                            k = ffn_bank(f"down{i}", b)
                            nc.vector.tensor_tensor(h3[:, i, :], down_part(b, i), expert_out[:, i, :],
                                                    ALU.add).then_inc(s_ffn_read[k], 1)
                            if b == B - 1:
                                ffn_read(dve, f"down{i}", b)
                                tile_variance(2, h3, i)
                                own(nc.vector.scalar_tensor_tensor(h3g[:, i, :], h3[:, i, :], mean_var[2][:, i, 0:1],
                                                                   gamma_sb[:, :], ALU.subtract, ALU.mult))
                        if b < B - 1:
                            for i in range(TT):
                                ffn_read(dve, f"down{i}", b)
                            statistics(2, h3)
                    for k, at in ((0, LN1), (1, LN2), (2, LN3), (3, LN4)):
                        if (mid, late, end, end)[k] == at + 1 and not (b == B - 1 and k >= 2):
                            variance(k)
                    if end == LN3 + 1 and b < B - 1:
                        for i in range(TT):
                            own(nc.vector.scalar_tensor_tensor(h3g[:, i, :], h3[:, i, :], mean_var[2][:, i, 0:1],
                                                               gamma_sb[:, :], ALU.subtract, ALU.mult))
                    if end == LN4 and b == B - 1:
                        dve.wait_ge(s_x2b, TT * (b + 1))
                        settle()
                        for i in range(TT):
                            dve.wait_ge(s_rstd, LN_USE[2, b] + i + 1)
                            own(nc.vector.scalar_tensor_tensor(h4[:, i, :], h3g[:, i, :], rstd[2][:, i:i + 1],
                                                               x2_beta[:, i, :], ALU.mult, ALU.add))
                            settle()
                            own(nc.vector.bn_stats(stats[3][:, i, :], h4[:, i, :]))
                        variance(3)
                    elif end == LN4:
                        dve.wait_ge(s_rstd, LN_USE[2, b] + 1)
                        dve.wait_ge(s_x2b, TT * (b + 1))
                        settle()
                        for i in range(TT):
                            own(nc.vector.scalar_tensor_tensor(h4[:, i, :], h3g[:, i, :], rstd[2][:, i:i + 1],
                                                               x2_beta[:, i, :], ALU.mult, ALU.add))
                        settle()
                        statistics(3, h4)
                    if end == LN4 + 3:
                        if b >= 1:
                            dve.wait_ge(s_store, 16 * b)
                        if b < B - 1:
                            normalise(3, b, h4, y_out, s_out)
                        else:
                            for i in range(TT):
                                dve.wait_ge(s_rstd, LN_USE[2, b] + TT + 1)
                                nc.vector.tensor_scalar(y_out[:, i, :], h4[:, i, :], mean_var[3][:, i, 0:1],
                                                        rstd[3][:, i:i + 1], ALU.subtract,
                                                        ALU.mult).then_inc(s_out, 1)


INPUTS = ["x", "ctx_2048", "L0_attn_Wq", "L0_attn_bq", "L0_attn_Wk", "L0_attn_bk", "L0_attn_Wv", "L0_attn_bv",
          "L0_attn_Wo", "L0_attn_bo", "L0_xattn_w", "L0_xattn_u", "L0_ffn_gate_w", "L0_ffn_up_w",
          "L0_ffn_down_w", "L0_ffn_expert_weight", "L0_ffn_ln_gamma", "L0_ffn_ln_beta"]


def kernel(**inputs):
    import concourse.bacc as bacc
    from concourse.bass_utils import run_bass_kernel_spmd

    nc = bacc.Bacc("TRN2", target_bir_lowering=False, num_devices=1)
    arrays, args = {}, []
    for name in INPUTS:
        a = np.ascontiguousarray(inputs[name])
        arrays[f"in_{name}"] = a
        args.append(nc.dram_tensor(f"in_{name}", a.shape, mybir.dt.from_np(a.dtype), kind="ExternalInput").ap())
    shape = arrays["in_x"].shape
    args.append(nc.dram_tensor("out_y", shape, mybir.dt.float32, kind="ExternalOutput").ap())
    decoder_layer(nc, *args)
    r = run_bass_kernel_spmd(nc, [arrays], core_ids=[0])
    return r.results[0]["out_y"]
```
